# Optimizing a Trainium2 kernel written in Bass

```python
import numpy as np
import jax
import jax.numpy as jnp

def _softmax(x, axis=-1):
    return jax.nn.softmax(x, axis=axis)

def _gelu(x):
    return jax.nn.gelu(x, approximate=True)

def _silu(x):
    return jax.nn.silu(x)

def _sigmoid(x):
    return jax.nn.sigmoid(x)

def _layernorm(x, axis=-1, eps=1e-05):
    m = jnp.mean(x, axis=axis, keepdims=True)
    v = jnp.var(x, axis=axis, keepdims=True)
    return (x - m) / jnp.sqrt(v + eps)

def _scatter_add(tgt, idx, src, axis=0):
    return tgt.at[idx].add(src)

def _segment_sum(src, seg, n):
    return jax.ops.segment_sum(src, seg, n)
kernel_name = 'mk_decoder_preln_d1_seqx_r4_7512d7'

def setup_inputs(seed: int=0):
    np.random.seed(seed)
    _w = jnp.asarray

    def _rec_inputs():
        import jax
        import jax.numpy as jnp
        _rk = jax.random.key(seed)
        x = 7.22e-05 + 1 * jax.random.normal(jax.random.fold_in(_rk, 1), (1, 2048, 256), jnp.float32)
        _lenS = 2048 - jax.random.randint(jax.random.fold_in(_rk, 7), (1,), 0, max(1, 2048 // 4) + 1, jnp.int32)
        _lenS2 = 1601 - jax.random.randint(jax.random.fold_in(_rk, 8), (1,), 0, max(1, 1601 // 4) + 1, jnp.int32)
        _ctx_1024P = jax.random.normal(jax.random.fold_in(_rk, 11), (1, 16, 256), jnp.float32)
        _ctx_1024c = jax.random.dirichlet(jax.random.fold_in(_rk, 511), 0.3 * jnp.ones((16,), jnp.float32), (1, 1601))
        _ctx_1024t = jnp.einsum('bsk,bkd->bsd', _ctx_1024c, _ctx_1024P)
        _ctx_1024t = _ctx_1024t * jax.lax.rsqrt(jnp.mean(jnp.square(_ctx_1024t)) + 1e-12) * 0.953939
        ctx_1024 = 4.13588e-05 + 0.999923 * (_ctx_1024t + 0.3 * jax.random.normal(jax.random.fold_in(_rk, 611), (1, 1601, 256), jnp.float32))
        return (x, ctx_1024)
    x, ctx_1024 = _rec_inputs()

    def _L0_attn_setup():
        import jax, jax.numpy as jnp
        import numpy as np
        _J6 = jnp.array([[0, 0, 0, 0, 0, 1], [0, 0, 0, 0, -1, 0], [0, 0, 0, 1, 0, 0], [0, 0, 1, 0, 0, 0], [0, -1, 0, 0, 0, 0], [1, 0, 0, 0, 0, 0]], dtype=jnp.float32)
        _PAIRS = [(0, 1), (0, 2), (0, 3), (1, 2), (1, 3), (2, 3)]
        _H = 16
        _SCALE = 6.0 ** (-0.5)

        def _plucker_lines(p1, p2):
            parts = [p1[..., i] * p2[..., j] - p1[..., j] * p2[..., i] for i, j in _PAIRS]
            lines = jnp.stack(parts, axis=-1)
            n = jnp.linalg.norm(lines, axis=-1, keepdims=True)
            return lines / jnp.maximum(n, 1e-12)
        key = jax.random.key(seed)
        ks = jax.random.split(key, 9)
        B, T, D, H = (2, 512, 256, _H)
        std = 0.02
        return {'x': jax.random.normal(ks[0], (B, T, D), jnp.float32), 'W1_q': jax.random.normal(ks[1], (4 * H, 2 * D), jnp.float32) * std, 'W2_q': jax.random.normal(ks[2], (4 * H, 2 * D), jnp.float32) * std, 'W1_k': jax.random.normal(ks[3], (4 * H, D), jnp.float32) * std, 'W2_k': jax.random.normal(ks[4], (4 * H, D), jnp.float32) * std, 'Wv': jax.random.normal(ks[5], (D, D), jnp.float32) * std, 'bv': jnp.zeros((D,), jnp.float32), 'Wo': jax.random.normal(ks[6], (D, D), jnp.float32) * std, 'bo': jnp.zeros((D,), jnp.float32)}
    _L0_attn_all = _L0_attn_setup()
    _L0_attn_in = {k: v for k, v in _L0_attn_all.items() if k in ('W1_q', 'W2_q', 'W1_k', 'W2_k', 'Wv', 'bv', 'Wo', 'bo')}
    del _L0_attn_all

    def _L0_xattn_setup():
        import jax, jax.numpy as jnp
        import numpy as np
        E = 256
        H = 16
        D = E // H

        def _split_heads(x):
            B, S, _ = x.shape
            return x.reshape(B, S, H, D).transpose(0, 2, 1, 3)
        key = jax.random.key(seed)
        ks = jax.random.split(key, 8)
        B, S = (4, 512)
        scale = 1.0 / np.sqrt(E)
        return {'Q': jax.random.normal(ks[0], (B, S, E), jnp.float32), 'K': jax.random.normal(ks[1], (B, S, E), jnp.float32), 'V': jax.random.normal(ks[2], (B, S, E), jnp.float32), 'Wq': jax.random.normal(ks[3], (E, E), jnp.float32) * scale, 'Wk': jax.random.normal(ks[4], (E, E), jnp.float32) * scale, 'Wv': jax.random.normal(ks[5], (E, E), jnp.float32) * scale, 'Wo': jax.random.normal(ks[6], (E, E), jnp.float32) * scale, 'bo': jax.random.normal(ks[7], (E,), jnp.float32) * 0.01}
    _L0_xattn_all = _L0_xattn_setup()
    _L0_xattn_in = {k: v for k, v in _L0_xattn_all.items() if k in ('Wq', 'Wk', 'Wv', 'Wo', 'bo')}
    del _L0_xattn_all

    def _L0_ffn_setup():
        import jax, jax.numpy as jnp
        import numpy as np
        B, N, D, E, DFF = (4, 512, 256, 16, 1024)
        CAPACITY_FACTOR = 2.0
        CAP = int(N * CAPACITY_FACTOR / E)
        SINKHORN_ITERS = 6

        def _sinkhorn(logits, n_iters=SINKHORN_ITERS, tau=1.0):
            t = logits / tau
            for _ in range(n_iters):
                t = t - jax.scipy.special.logsumexp(t, axis=-2, keepdims=True)
                t = t - jax.scipy.special.logsumexp(t, axis=-1, keepdims=True)
            return jnp.exp(t)
        key = jax.random.key(seed)
        ks = jax.random.split(key, 6)
        scaled = lambda k, sh, fan: (jax.random.normal(k, sh, jnp.float32) / np.sqrt(fan)).astype(jnp.float32)
        return {'x': jax.random.normal(ks[0], (B, N, D), jnp.float32), 'gate_query': scaled(ks[1], (E, D), D), 'log_temp': jnp.asarray(np.log(0.5), jnp.float32), 'w1': scaled(ks[2], (E, D, DFF), D), 'b1': jnp.zeros((E, DFF), jnp.float32), 'w2': scaled(ks[3], (E, DFF, D), DFF), 'b2': jnp.zeros((E, D), jnp.float32)}
    _L0_ffn_all = _L0_ffn_setup()
    _L0_ffn_in = {k: v for k, v in _L0_ffn_all.items() if k in ('gate_query', 'log_temp', 'w1', 'b1', 'w2', 'b2')}
    del _L0_ffn_all
    return {'x': x, 'ctx_1024': ctx_1024, 'L0_attn_W1_q': _L0_attn_in['W1_q'], 'L0_attn_W2_q': _L0_attn_in['W2_q'], 'L0_attn_W1_k': _L0_attn_in['W1_k'], 'L0_attn_W2_k': _L0_attn_in['W2_k'], 'L0_attn_Wv': _L0_attn_in['Wv'], 'L0_attn_bv': _L0_attn_in['bv'], 'L0_attn_Wo': _L0_attn_in['Wo'], 'L0_attn_bo': _L0_attn_in['bo'], 'L0_xattn_Wq': _L0_xattn_in['Wq'], 'L0_xattn_Wk': _L0_xattn_in['Wk'], 'L0_xattn_Wv': _L0_xattn_in['Wv'], 'L0_xattn_Wo': _L0_xattn_in['Wo'], 'L0_xattn_bo': _L0_xattn_in['bo'], 'L0_ffn_gate_query': _L0_ffn_in['gate_query'], 'L0_ffn_log_temp': _L0_ffn_in['log_temp'], 'L0_ffn_w1': _L0_ffn_in['w1'], 'L0_ffn_b1': _L0_ffn_in['b1'], 'L0_ffn_w2': _L0_ffn_in['w2'], 'L0_ffn_b2': _L0_ffn_in['b2']}

def reference(x, ctx_1024, L0_attn_W1_q, L0_attn_W2_q, L0_attn_W1_k, L0_attn_W2_k, L0_attn_Wv, L0_attn_bv, L0_attn_Wo, L0_attn_bo, L0_xattn_Wq, L0_xattn_Wk, L0_xattn_Wv, L0_xattn_Wo, L0_xattn_bo, L0_ffn_gate_query, L0_ffn_log_temp, L0_ffn_w1, L0_ffn_b1, L0_ffn_w2, L0_ffn_b2):
    import jax
    import jax.numpy as jnp

    def _L0_attn_ref(x, W1_q, W2_q, W1_k, W2_k, Wv, bv, Wo, bo):
        import jax, jax.numpy as jnp
        import numpy as np
        _J6 = jnp.array([[0, 0, 0, 0, 0, 1], [0, 0, 0, 0, -1, 0], [0, 0, 0, 1, 0, 0], [0, 0, 1, 0, 0, 0], [0, -1, 0, 0, 0, 0], [1, 0, 0, 0, 0, 0]], dtype=jnp.float32)
        _PAIRS = [(0, 1), (0, 2), (0, 3), (1, 2), (1, 3), (2, 3)]
        _H = 16
        _SCALE = 6.0 ** (-0.5)

        def _plucker_lines(p1, p2):
            parts = [p1[..., i] * p2[..., j] - p1[..., j] * p2[..., i] for i, j in _PAIRS]
            lines = jnp.stack(parts, axis=-1)
            n = jnp.linalg.norm(lines, axis=-1, keepdims=True)
            return lines / jnp.maximum(n, 1e-12)
        B, T, D = x.shape
        H = _H
        dh = D // H
        x_prev = jnp.pad(x[:, :-1, :], ((0, 0), (1, 0), (0, 0)))
        bg = jnp.concatenate([x, x_prev], axis=-1)
        q1 = (bg @ W1_q.T).reshape(B, T, H, 4)
        q2 = (bg @ W2_q.T).reshape(B, T, H, 4)
        k1 = (x @ W1_k.T).reshape(B, T, H, 4)
        k2 = (x @ W2_k.T).reshape(B, T, H, 4)
        q = _plucker_lines(q1, q2).transpose(0, 2, 1, 3)
        k = _plucker_lines(k1, k2).transpose(0, 2, 1, 3)
        Jk = k @ _J6.T
        logits = jnp.einsum('bhtc,bhsc->bhts', q, Jk) * _SCALE
        causal = jnp.tril(jnp.ones((T, T), dtype=bool))
        logits = jnp.where(causal[None, None], logits, -jnp.inf)
        attn = jax.nn.softmax(logits, axis=-1)
        v = (x @ Wv.T + bv).reshape(B, T, H, dh).transpose(0, 2, 1, 3)
        o = jnp.einsum('bhts,bhsd->bhtd', attn, v)
        o = o.transpose(0, 2, 1, 3).reshape(B, T, D)
        return o @ Wo.T + bo

    def _L0_xattn_ref(Q, K, V, Wq, Wk, Wv, Wo, bo):
        import jax, jax.numpy as jnp
        import numpy as np
        E = 256
        H = 16
        D = E // H

        def _split_heads(x):
            B, S, _ = x.shape
            return x.reshape(B, S, H, D).transpose(0, 2, 1, 3)
        q = _split_heads(Q @ Wq.T)
        k = _split_heads(K @ Wk.T)
        v = _split_heads(V @ Wv.T)
        scores = jnp.einsum('bhqd,bhkd->bhqk', q, k)
        attn = jax.nn.softmax(scores, axis=-1)
        out = jnp.einsum('bhqk,bhkd->bhqd', attn, v)
        B, _, Sq, _ = out.shape
        out = out.transpose(0, 2, 1, 3).reshape(B, Sq, E)
        return out @ Wo.T + bo

    def _L0_ffn_ref(x, gate_query, log_temp, w1, b1, w2, b2):
        import jax, jax.numpy as jnp
        import numpy as np
        B, N, D, E, DFF = (4, 512, 256, 16, 1024)
        CAPACITY_FACTOR = 2.0
        CAP = int(N * CAPACITY_FACTOR / E)
        SINKHORN_ITERS = 6

        def _sinkhorn(logits, n_iters=SINKHORN_ITERS, tau=1.0):
            t = logits / tau
            for _ in range(n_iters):
                t = t - jax.scipy.special.logsumexp(t, axis=-2, keepdims=True)
                t = t - jax.scipy.special.logsumexp(t, axis=-1, keepdims=True)
            return jnp.exp(t)
        b, n, d = x.shape
        gate_logits = jnp.einsum('bnd,ed->ben', x, gate_query)
        affinity_logits = gate_logits / jnp.exp(log_temp)
        affinity = _sinkhorn(affinity_logits)
        gates, idx = jax.lax.top_k(affinity, CAP)
        expert_in = jnp.take_along_axis(x[:, None, :, :], idx[..., None], axis=2)
        h = jax.nn.gelu(jnp.einsum('becd,edf->becf', expert_in, w1) + b1[None, :, None, :])
        expert_out = jnp.einsum('becf,efd->becd', h, w2) + b2[None, :, None, :]
        out = jnp.zeros_like(x)
        out = out.at[jnp.arange(b)[:, None, None], idx].add(gates[..., None] * expert_out)
        return out
    x = x + _L0_attn_ref(_layernorm(x, axis=-1), L0_attn_W1_q, L0_attn_W2_q, L0_attn_W1_k, L0_attn_W2_k, L0_attn_Wv, L0_attn_bv, L0_attn_Wo, L0_attn_bo)
    x = x + _L0_xattn_ref(_layernorm(x, axis=-1), ctx_1024, ctx_1024, L0_xattn_Wq, L0_xattn_Wk, L0_xattn_Wv, L0_xattn_Wo, L0_xattn_bo)
    x = x + _L0_ffn_ref(_layernorm(x, axis=-1), L0_ffn_gate_query, L0_ffn_log_temp, L0_ffn_w1, L0_ffn_b1, L0_ffn_w2, L0_ffn_b2)
    return x

_drawn_inputs = setup_inputs


def setup_inputs(seed=0):
    import zlib

    import numpy as np

    out = dict(_drawn_inputs(seed))
    spreads = {'L0_attn_bv': (0.0, 0.1),
     'L0_attn_bo': (0.0, 0.1),
     'L0_ffn_b1': (0.0, 2.0),
     'L0_ffn_b2': (0.0, 2.0)}
    factors = {'L0_attn_W1_q': 23.599,
     'L0_attn_W2_q': 8.0,
     'L0_attn_W1_k': 8.0,
     'L0_attn_W2_k': 24.972,
     'L0_attn_Wv': 7.435,
     'L0_xattn_bo': 7.726,
     'L0_ffn_gate_query': 8.0,
     'L0_ffn_w1': 8.0,
     'L0_ffn_w2': 8.0}
    for name, (base, spread) in spreads.items():
        noise = np.random.default_rng([zlib.crc32(name.encode()), seed]).standard_normal(out[name].shape)
        drawn = base * np.exp(spread * noise) if base else spread * noise
        out[name] = jnp.asarray(drawn.astype(out[name].dtype))
    for name, factor in factors.items():
        out[name] = (out[name] * factor).astype(out[name].dtype)
    return out
```

```python
from contextlib import ExitStack

import concourse.bass as bass
from concourse import mybir

F32 = mybir.dt.float32
BF16 = mybir.dt.bfloat16
U32 = mybir.dt.uint32
ALU = mybir.AluOpType
ACT = mybir.ActivationFunctionType
AX_X = mybir.AxisListType.X

P = 128
T = 2048
D = 256
DK = D // P
S = 1601
H = 16
DH = D // H
VW = DH + 1
VB = H * VW + (32 - VW)
VP = 288
NC = 6
TB = T // P
TILE = 512
NT = T // TILE
BPT = TILE // P
SB = -(-S // P)
SP = 1604
ST = -(-S // TILE)
E = 16
CAP = 64
FF = 1024
NSLOT = 8
EPS = 1e-5
SINK_ITERS = 6
LSCALE = 6.0 ** -0.5
Q_PAIRS = [(0, 1), (0, 2), (0, 3), (1, 2), (1, 3), (2, 3)]
K_PAIRS = [(2, 3), (3, 1), (1, 2), (0, 3), (2, 0), (0, 1)]
Q_SLOTS = (0, 1, 0, 1, 2, 0)
K_SLOTS = (0, 0, 1, 1, 0, 2)
NS = len(Q_SLOTS)


def weave(steps, fill):
    out, done = [], 0
    for i, s in enumerate(steps):
        upto = len(fill) * (i + 1) // len(steps)
        out += [s] + fill[done:upto]
        done = upto
    return [s for s in out if s[0] != "gap"]


def build_plan():
    quads, w = [], [0]

    def attend(kind, j):
        out = []
        for g in range(4):
            blocks = BPT * (j + 1) if kind == "self" else SB
            for i in range(blocks):
                n = len(quads)
                quads.append((kind, j, g, i, i == blocks - 1))
                step = [("scores", n)]
                if n:
                    step += [("pv", n - 1)]
                    k, jj, gg, _, end = quads[n - 1]
                    if end:
                        step += [("o_evac", k, jj, gg, n - 1)]
                out.append(step)
        return out

    def load_x(kind, j):
        use = []
        for b in range(BPT * j, BPT * j + BPT):
            use.append((b, w[0]))
            w[0] += 1
        return use

    def norm_steps(use, kind):
        s = [("x_load", kind, b, u) for b, u in use]
        s += [("stats", kind, b, u) for b, u in use]
        return s

    def prep(j):
        use = load_x("prep", j)
        s = norm_steps(use, "prep") + [("carry", j)]
        for n, (b, u) in enumerate(use):
            s += [("norm", "prep", b, u), ("x_turn", "prep", b, u)]
            if n:
                s += [("project", use[n - 1][0])]
        s += [("project", use[-1][0]), ("carry_out", j), ("lines_a", j), ("gap",), ("gap",), ("lines_b", j)]
        s += [("line_turn", b) for b, _ in use] + [("line_load", j)]
        return s

    def join(kind, j):
        use = load_x(kind, j)
        s = [("x_load", kind, b, u) for b, u in use]
        for n in range(len(use) + 1):
            if n:
                s += [("a_turn", kind, *use[n - 1])]
            if n < len(use):
                s += [("o_turn", kind, *use[n])]
            if n:
                s += [("out_proj", kind, *use[n - 1])]
        if kind == "cross":
            for b, u in use:
                s += [("norm", "cross", b, u), ("x_turn", "cross", b, u)]
            s += [("gate", b) for b, _ in use]
        return s

    def query(j):
        use = load_x("query", j)
        s = norm_steps(use, "query") + [("gap",)]
        for b, u in use:
            s += [("norm", "query", b, u), ("x_turn", "query", b, u)]
        s += [("x_query", j, m) for m in range(DK)] + [("query_load", j)] + [("gap",)] * 10
        for b, _ in use:
            s += [("max", j, b, h, c) for h in range(H) for c in range(ST)]
            s += [("shift", j, b), ("shift_turn", j, b)]
        return s + [("shift_load", j)] + [("gap",)] * 3

    ctx = []
    for t in range(ST):
        ctx += [("ctx_k", t, 0), ("ctx_k", t, 1)]
        ctx += [("ctx_v", b) for b in range(BPT * t, min(BPT * t + BPT, SB), 2)]
        ctx += [("ctx_load", t)]
    p0 = prep(0)
    at, cut = p0.index(("carry", 0)), p0.index(("line_load", 0))
    plan = p0[:at] + weave(p0[at:cut], ctx) + p0[cut:]

    def run(steps, fill):
        for s in weave([("quad", s) for s in steps], fill):
            if s[0] == "quad":
                plan.extend(s[1])
            else:
                plan.append(s)

    run(attend("self", 0), prep(1))
    sa1 = attend("self", 1)
    run(sa1[:7], [("gap",)] * 2 + join("self", 0))
    run(sa1[7:], prep(2) + prep(3))
    j1 = join("self", 1)
    sa2 = attend("self", 2)
    q0 = query(0)
    run(sa2[:12], [("gap",)] * 2 + j1)
    run(sa2[12:], q0[:len(q0) * 36 // 100])
    j2 = join("self", 2)
    sa3 = attend("self", 3)
    run(sa3[:14], [("gap",)] * 2 + j2)
    run(sa3[14:], q0[len(q0) * 36 // 100:])
    for j in range(NT):
        xa = attend("cross", j)
        run(xa[:12], [("gap",)] * 2 + (join("self", 3) if j == 0 else join("cross", j - 1)))
        fill = query(j + 1) if j < NT - 1 else []
        if j == 0:
            fill += [("weights", e) for e in range(3)]
        run(xa[12:], fill)
    plan += [("pv", len(quads) - 1), ("o_evac", "cross", NT - 1, 3, len(quads) - 1)]
    plan += join("cross", NT - 1)
    g_use = {}
    G_STEPS = ("ctx_k", "ctx_v", "x_turn", "project", "line_turn", "o_turn", "a_turn", "out_proj", "x_query", "max",
               "shift_turn", "gate")
    for s in plan:
        if s[0] in G_STEPS:
            assert s not in g_use
            g_use[s] = len(g_use)
    return plan, quads, g_use


def decoder_layer(nc, x, ctx_t, w_self, w_o, w_xq, w_xk, w_xv, w_xo, bv, bo, xbo, gate_t, log_temp, w1, b1, w2, b2, out):
    PLAN, QUADS, G_USE = build_plan()
    n_plan = len(PLAN)
    where = {s: n for n, s in enumerate(PLAN)}

    line_d = nc.dram_tensor("line_d", (2, 3, H * NC, T), BF16, kind="Internal").ap()
    xk_d = nc.dram_tensor("xk_d", (3, D, SP), BF16, kind="Internal").ap()
    xq_d = nc.dram_tensor("xq_d", (3, D, T), BF16, kind="Internal").ap()
    shift_d = nc.dram_tensor("shift_d", (3, H, T), BF16, kind="Internal").ap()
    x1_d = nc.dram_tensor("x1_d", (T, D), F32, kind="Internal").ap()
    xn_d = nc.dram_tensor("xn_d", (T, D), F32, kind="Internal").ap()

    ctx = ExitStack()
    with ctx:
        def sb(name, shape, dt=F32):
            return ctx.enter_context(nc.sbuf_tensor(name, shape, dt))

        def sem(name):
            return ctx.enter_context(nc.semaphore(name))

        self_region = sb("self_region", [P, 16896])
        k_line = self_region[:, 0:8192].bitcast(BF16).rearrange("p (a t) -> p a t", a=8)
        v_self = self_region[:, 8192:8192 + TB * VP].rearrange("p (b v) -> p b v", b=TB)
        q_line = [self_region[:, 12800 + 2048 * r:14848 + 2048 * r].bitcast(BF16).rearrange("p (a t) -> p a t", a=8)
                  for r in range(2)]
        ctx_sb = self_region[:, 0:DK * S].rearrange("p (k s) -> p k s", k=DK)
        cross_region = sb("cross_region", [P, H * SP // 2 + SB * VP])
        k_cross = cross_region[:, 0:H * SP // 2].bitcast(BF16).rearrange("p (h s) -> p h s", h=H)
        v_cross = cross_region[:, H * SP // 2:].rearrange("p (b v) -> p b v", b=SB)
        probs = sb("probs", [P, 4, 2, TILE])
        even_region = sb("even_region", [P, 4096])
        raw = even_region[:, 0:1024].rearrange("p (b n) -> p b n", b=BPT)
        lines = even_region[:, 1024:1792].rearrange("p (s h c) -> p s h c", s=8, h=H)
        lines_t = even_region[:, 1792:2560].rearrange("p (s h c) -> p s h c", s=8, h=H)
        line_parts = even_region[:, 2560:3712].bitcast(BF16).rearrange("p (s q n) -> p s q n", s=8, q=3)
        line_n2 = even_region[:, 3712:3840]
        line_rn = even_region[:, 3840:3968]
        q_cross = [even_region[:, 0:4096].bitcast(BF16).rearrange("p (h t) -> p h t", h=H),
                   self_region[:, 0:4096].bitcast(BF16).rearrange("p (h t) -> p h t", h=H)]
        slots = [self_region[:, 4096 * (s + 1):4096 * (s + 2)] for s in range(3)]
        slots += [cross_region[:, 4096 * s:4096 * (s + 1)] for s in range(4)]
        slots += [probs[:, :, :, :].rearrange("p a b c -> p (a b c)")]

        o_region = sb("o_region", [P, 4 * TILE])
        o_sb = o_region[:, :].rearrange("p (g t) -> p g t", g=4)
        wxk_sb = o_region[:, 0:512].rearrange("p (k n) -> p k n", k=DK)
        wxv_sb = o_region[:, 512:1024].rearrange("p (k n) -> p k n", k=DK)
        xn_t = sb("xn_t", [P, DK, TILE + 1])
        carry = sb("carry", [P, DK])
        xb = sb("xb", [P, 4, D])
        xn = sb("xn", [P, 2, D])
        bn = sb("bn", [P, 4, 6])
        mv = sb("mv", [P, 4, 2])
        rstd = sb("rstd", [P, 4])
        attn = sb("attn", [P, D])
        rsum = sb("rsum", [P, H])
        attn_t = sb("attn_t", [P, DK, P])
        late_region = sb("late_region", [P, 384])
        line_t = late_region[0:H * NC, :].bitcast(BF16).rearrange("p (a t) -> p a t", a=6)
        wself_sb = sb("wself_sb", [P, DK, 640])
        parts_a = sb("parts_a", [P, 3, TILE], BF16)
        rest = sb("rest", [P, TILE])
        shift_parts = sb("shift_parts", [P, 3, H], BF16)
        shift_t = sb("shift_t", [3 * H, TILE], BF16)
        shift_f = sb("shift_f", [P, 2, H])
        mx = sb("mx", [P, 2, H, ST])
        wo_sb = sb("wo_sb", [P, DK, D])
        wxq_sb = sb("wxq_sb", [P, DK, D])
        wxo_sb = sb("wxo_sb", [P, DK, D])
        gate_sb = sb("gate_sb", [P, DK, E])
        bv_sb = sb("bv_sb", [P, D])
        bo_sb = sb("bo_sb", [P, D])
        xbo_sb = sb("xbo_sb", [P, D])
        ident = sb("ident", [P, P])
        identb = sb("identb", [P, P], BF16)
        half = sb("half", [P, P])
        parts_ctx = [parts_a[:, :, :],
                     self_region[:, 3328:4096].bitcast(BF16).rearrange("p (q t) -> p q t", q=3)]
        parts_q = [parts_a[:, :, :],
                   wself_sb[:, :, :].rearrange("p k n -> p (k n)")[:, 0:768].bitcast(BF16)
                   .rearrange("p (q t) -> p q t", q=3)]
        logits = sb("logits", [P, TB, E])
        wself_flat = wself_sb[:, :, :].rearrange("p k n -> p (k n)")
        sink = wself_flat[:, 768:1024].rearrange("p (b e) -> p b e", b=TB)
        turned = wself_flat[0:E, 1024:1280].rearrange("p (a n) -> p a n", a=2)
        ones = late_region[:, 0:P]
        tmp16 = late_region[:, P:P + 4 * E].rearrange("p (a e) -> p a e", a=4)
        temp = sb("temp", [P, 2])
        affin = logits
        affinity = o_region[0:E, :]
        tops = shift_t[0:E, :].bitcast(F32)[:, 0:3 * CAP].rearrange("p (a n) -> p a n", a=3)
        gates = sb("gates", [P, E // 2])
        idx_gather = sb("idx_gather", [P, E // 2], U32)
        idx_scatter = sb("idx_scatter", [CAP, E], U32)
        h_sb = [even_region[:, 0:1024], self_region[:, 0:1024]]
        h_t = [even_region[:, 1024:2048], self_region[:, 1024:2048]]
        b1_sb = [even_region[:, 2048:3072], even_region[:, 3072:4096]]
        x_e = [self_region[:, 2048 + 256 * r:2304 + 256 * r] for r in range(2)]
        x_et = [self_region[:, 2560 + 256 * r:2816 + 256 * r].rearrange("p (k n) -> p k n", k=DK) for r in range(2)]
        y_e = [self_region[:, 3072 + 256 * r:3328 + 256 * r] for r in range(4)]
        b2_sb = [o_region[:, 256 * r:256 * r + 256] for r in range(2)]

        ps = [ctx.enter_context(nc.psum_tensor(f"scores{r}", [P, 2, TILE], F32)) for r in range(2)]
        po = ctx.enter_context(nc.psum_tensor("po", [P, TILE], F32))
        pg = [ctx.enter_context(nc.psum_tensor(f"g{r}", [P, TILE], F32)) for r in range(3)]

        s_w = {n: sem(f"w_{n}") for n in ("ctx", "xk", "xv", "self", "rest")}
        const_ready = sem("const_ready")
        v_ones = sem("v_ones")
        g_full = sem("g_full")
        g_free = sem("g_free")
        dve_step = sem("dve_step")
        scores_full = sem("scores_full")
        exp_done = sem("exp_done")
        mask_done = sem("mask_done")
        pv_done = sem("pv_done")
        o_free = sem("o_free")
        x_loaded = [sem(f"x_loaded{r}") for r in range(4)]
        x_biased = sem("x_biased")
        x_stored = [sem(f"x_stored{r}") for r in range(4)]
        var_ready = sem("var_ready")
        rstd_ready = sem("rstd_ready")
        xn_ready = sem("xn_ready")
        xn_stored = [sem(f"xn_stored{r}") for r in range(2)]
        n2_ready = sem("n2_ready")
        rn_ready = sem("rn_ready")
        lines_split = sem("lines_split")
        line_stored = sem("line_stored")
        lines_loaded = [sem(f"lines_loaded{j}") for j in range(NT)]
        parts_ready = sem("parts_ready")
        parts_stored = [sem(f"parts_stored{r}") for r in range(2)]
        ctx_loaded = sem("ctx_loaded")
        query_loaded = [sem(f"query_loaded{j}") for j in range(NT)]
        shift_split = sem("shift_split")
        shift_stored = sem("shift_stored")
        shift_loaded = [sem(f"shift_loaded{j}") for j in range(NT)]
        temp_ready = sem("temp_ready")
        sink_ready = sem("sink_ready")
        sink_act = sem("sink_act")
        router_pe = sem("router_pe")
        picked = sem("picked")
        gathered = [sem(f"gathered{r}") for r in range(2)]
        bias_loaded = [sem(f"bias_loaded{r}") for r in range(2)]
        h_turned = sem("h_turned")
        gelu_done = sem("gelu_done")
        y_ready = sem("y_ready")
        scattered = sem("scattered")
        slot_loaded = [sem(f"slot_loaded{s}") for s in range(NSLOT)]

        def g_at(step):
            return G_USE[step]

        loads = {}
        for st in PLAN:
            if st[0] == "x_load":
                loads[st[3]] = st

        def count_before(test, step):
            return sum(1 for s in PLAN[:where[step]] if test(s))

        splits = [s for s in PLAN if s[0] in ("ctx_k", "x_query")]
        norms = [s for s in PLAN if s[0] == "norm"]
        stats = [(s[1], s[2], s[3]) for s in PLAN if s[0] == "stats" or (s[0] == "out_proj" and s[1] == "cross")]
        joins = [s for s in PLAN if s[0] == "out_proj"]
        biased = [s for s in PLAN if s[0] == "x_load" and s[1] in ("self", "cross")]
        masks = [n for n, (kind, j, g, i, _) in enumerate(QUADS) if kind == "self" and i >= BPT * j]
        norm_no = {s[3]: n for n, s in enumerate(norms)}
        stat_no = {s[2]: n for n, s in enumerate(stats)}
        join_no = {s[3]: n for n, s in enumerate(joins)}
        bias_no = {s[3]: n for n, s in enumerate(biased)}
        mask_no = {n: m for m, n in enumerate(masks)}
        last_quad = {}
        for n, (kind, j, g, i, end) in enumerate(QUADS):
            last_quad[kind, j] = n
        evacs = [s for s in PLAN if s[0] == "o_evac"]
        x_stores = [sum(1 for s in joins if s[3] % 4 == r) for r in range(4)]
        evac_no = {(s[1], s[2], s[3]): n for n, s in enumerate(evacs)}

        def quad_cols(n):
            kind, j, g, i, _ = QUADS[n]
            off = max(0, i - BPT * j) * P if kind == "self" else 0
            rows = min(P, S - i * P) if kind == "cross" else P
            return off, rows

        ctx_users = [g_at(s) for s in PLAN if s[0] in ("ctx_k", "ctx_v")]

        NG = len(G_USE)
        tail = ["col_turn", "col_back"] + [("col_sum", it) for it in range(SINK_ITERS)]
        tail += [("aff", c) for c in range(4)] + ["tops", ("xe", 0), ("h", 0, 0), ("h", 0, 1)]
        for i in range(E // 2):
            if i + 1 < E // 2:
                tail += [("xe", i + 1), ("h", i + 1, 0), ("h", i + 1, 1)]
            tail += [("y", i)]
        TG = {s: NG + n for n, s in enumerate(tail)}

        def tail_full(dve, name):
            dve.wait_ge(g_full, TG[name] + 1)
            return pg[TG[name] % 3]

        def tail_bank(pe, name):
            pe.wait_ge(g_free, TG[name] - 2)
            return pg[TG[name] % 3]

        def load_expert(eng, e):
            s = e % NSLOT
            eng.dma_start(slots[s][:, 0:2048].rearrange("p (k n) -> p k n", k=2),
                          w1[e].rearrange("(k p) n -> p k n", p=P)).then_inc(slot_loaded[s], 16)
            eng.dma_start(slots[s][:, 2048:4096].rearrange("p (k n) -> p k n", k=8),
                          w2[e].rearrange("(k p) n -> p k n", p=P)).then_inc(slot_loaded[s], 16)

        block = ctx.enter_context(nc.Block())

        @block.sync
        def _(sp):
            sp.dma_start(wself_sb[:, :, :], w_self.rearrange("(k p) n -> p k n", p=P)).then_inc(s_w["self"], 16)
            stored = {}
            store_count = [0] * 4
            line_stores = 0
            n_parts = [0, 0]
            shift_stores = 0
            xn_store_count = [0, 0]

            def plain_load(step):
                _, kind, b, u = step
                r = u % 4
                if u >= 4:
                    prev = loads[u - 4]
                    if prev[1] != "self":
                        sp.wait_ge(xn_ready, norm_no[u - 4] + 1)
                    if prev[1] in ("self", "cross"):
                        sp.wait_ge(x_stored[r], 16 * store_count[r])
                src = x if kind in ("prep", "self") else x1_d
                if kind in ("query", "cross"):
                    us, cnt = stored[b]
                    sp.wait_ge(x_stored[us % 4], 16 * cnt)
                sp.dma_start(xb[:, r, :], src[b * P:(b + 1) * P, :]).then_inc(x_loaded[r], 16)

            for step in PLAN:
                kind = step[0]
                if kind == "x_load":
                    plain_load(step)
                elif kind == "stats" and step[3] == 0:
                    sp.dma_start(ctx_sb, ctx_t.rearrange("(k p) s -> p k s", p=P)).then_inc(s_w["ctx"], 16)
                    sp.dma_start(wxk_sb, w_xk.rearrange("(k p) n -> p k n", p=P)).then_inc(s_w["xk"], 16)
                    sp.dma_start(wxv_sb, w_xv.rearrange("(k p) n -> p k n", p=P)).then_inc(s_w["xv"], 16)
                    for dst, src in ((wo_sb, w_o), (wxq_sb, w_xq), (wxo_sb, w_xo)):
                        sp.dma_start(dst[:, :, :], src.rearrange("(k p) n -> p k n", p=P)).then_inc(s_w["rest"], 16)
                    sp.dma_start(gate_sb[:, :, :], gate_t.rearrange("(k p) n -> p k n", p=P)).then_inc(s_w["rest"], 16)
                    for dst, src in ((bv_sb, bv), (bo_sb, bo), (xbo_sb, xbo)):
                        sp.dma_start(dst[:, :], src.partition_broadcast(P)).then_inc(s_w["rest"], 16)
                    sp.dma_start(temp[:, 0:1], log_temp.partition_broadcast(P)).then_inc(s_w["rest"], 16)
                elif kind in ("ctx_k", "x_query"):
                    n = splits.index(step)
                    r = n % 2
                    sp.wait_ge(parts_ready, n + 1)
                    if kind == "ctx_k":
                        _, t, m = step
                        n_keys = min(TILE, S - t * TILE)
                        dst = xk_d[:, m * P:(m + 1) * P, t * TILE:t * TILE + n_keys]
                        src = parts_ctx[r][:, :, 0:n_keys]
                    else:
                        _, j, m = step
                        dst = xq_d[:, m * P:(m + 1) * P, j * TILE:(j + 1) * TILE]
                        src = parts_q[r]
                    sp.dma_start(dst.rearrange("q p n -> p q n"), src).then_inc(parts_stored[r], 16)
                    n_parts[r] += 1
                elif kind == "ctx_load":
                    t = step[1]
                    n_keys = min(TILE, S - t * TILE)
                    for r in range(2):
                        sp.wait_ge(parts_stored[r], 16 * n_parts[r])
                    for s, part in enumerate(K_SLOTS):
                        sp.dma_start(k_cross[s * DH:(s + 1) * DH, :, t * TILE:t * TILE + n_keys],
                                     xk_d[part, :, t * TILE:t * TILE + n_keys].rearrange("(h d) n -> d h n", d=DH)
                                     ).then_inc(ctx_loaded, 16)
                elif kind == "query_load":
                    j = step[1]
                    for r in range(2):
                        sp.wait_ge(parts_stored[r], 16 * n_parts[r])
                    if j == 1:
                        sp.wait_ge(pv_done, last_quad["self", NT - 1] + 1)
                    if j >= 2:
                        sp.wait_ge(pv_done, last_quad["cross", j - 2] + 1)
                    for s, part in enumerate(Q_SLOTS):
                        sp.dma_start(q_cross[j % 2][s * DH:(s + 1) * DH, :, :],
                                     xq_d[part, :, j * TILE:(j + 1) * TILE].rearrange("(h d) n -> d h n", d=DH)
                                     ).then_inc(query_loaded[j], 16)
                elif kind == "line_turn":
                    b = step[1]
                    sp.wait_ge(g_free, g_at(step) + 1)
                    sp.dma_start(line_d[:, :, :, b * P:(b + 1) * P].rearrange("a q n t -> n (a q) t"),
                                 line_t[:, :, :]).then_inc(line_stored, 16)
                    line_stores += 1
                elif kind == "line_load":
                    j = step[1]
                    sp.wait_ge(line_stored, 16 * line_stores)
                    if j == 0:
                        sp.wait_ge(g_free, max(g_at(s) for s in PLAN if s[0] in ("ctx_k", "ctx_v")) + 1)
                        for r in range(2):
                            sp.wait_ge(parts_stored[r], 16 * n_parts[r])
                    if j >= 2:
                        sp.wait_ge(pv_done, last_quad["self", j - 2] + 1)
                    for side, slots_of, dst in ((0, Q_SLOTS, q_line[j % 2][:, :, :]),
                                                (1, K_SLOTS, k_line[:, :, j * TILE:(j + 1) * TILE])):
                        for s, part in enumerate(slots_of):
                            src = line_d[side, part, :, j * TILE:(j + 1) * TILE].rearrange(
                                "(a e c) t -> c e a t", e=2, c=NC)
                            for e in range(2):
                                sp.dma_start(dst[64 * e + s * NC:64 * e + (s + 1) * NC, :, :],
                                             src[:, e, :, :]).then_inc(lines_loaded[j], 16)
                elif kind == "out_proj":
                    _, which, b, u = step
                    r = u % 4
                    sp.wait_ge(g_free, g_at(step) + 1)
                    sp.dma_start((x1_d if which == "self" else out)[b * P:(b + 1) * P, :],
                                 xb[:, r, :]).then_inc(x_stored[r], 16)
                    store_count[r] += 1
                    if which == "self":
                        stored[b] = (u, store_count[r])
                elif kind == "norm" and step[1] == "cross":
                    _, _, b, u = step
                    r = norm_no[u] % 2
                    sp.wait_ge(xn_ready, norm_no[u] + 1)
                    sp.dma_start(xn_d[b * P:(b + 1) * P, :], xn[:, r, :]).then_inc(xn_stored[r], 16)
                    xn_store_count[r] += 1
                elif kind == "shift_load":
                    j = step[1]
                    sp.wait_ge(g_free, g_at(("shift_turn", j, BPT * j + BPT - 1)) + 1)
                    cols = slice(j * TILE, (j + 1) * TILE)
                    sp.dma_start(shift_d[:, :, cols].rearrange("q h t -> (q h) t"),
                                 shift_t[:, :]).then_inc(shift_stored, 16)
                    shift_stores += 1
                    sp.wait_ge(shift_stored, 16 * shift_stores)
                    sp.dma_start(q_cross[j % 2][NS * DH:NS * DH + 3, :, :],
                                 shift_d[:, :, cols]).then_inc(shift_loaded[j], 16)
            for r in range(4):
                sp.wait_ge(x_stored[r], 16 * store_count[r])
            for r in range(2):
                sp.wait_ge(xn_stored[r], 16 * xn_store_count[r])
            sp.wait_ge(pv_done, len(QUADS))
            for i in range(E // 2):
                if i == 0:
                    sp.wait_ge(g_free, TG["tops"] + 1)
                if i >= 2:
                    sp.wait_ge(g_free, TG["y", i - 2] + 1)
                for e in range(2):
                    rows = slice(CAP * e, CAP * (e + 1))
                    sp.dma_start(b1_sb[i % 2][rows, :], b1[2 * i + e].partition_broadcast(CAP)
                                 ).then_inc(bias_loaded[i % 2], 16)
                    sp.dma_start(b2_sb[i % 2][rows, :], b2[2 * i + e].partition_broadcast(CAP)
                                 ).then_inc(bias_loaded[i % 2], 16)
                if i >= 2 and 2 * (i - 2) + NSLOT < E:
                    sp.wait_ge(g_full, TG["y", i - 2] + 1)
                    for e in range(2):
                        load_expert(sp, 2 * (i - 2) + e + NSLOT)

        @block.gpsimd
        def _(pool):
            pool.memset(half[:, :], -0.5).then_inc(const_ready, 1)
            pool.memset(ident[:, :], 0.0).then_inc(const_ready, 1)
            pool.memset(identb[:, :], 0.0).then_inc(const_ready, 1)
            pool.wait_ge(const_ready, 3)
            for m in (ident, identb):
                pool.affine_select(out=m[:, :], in_=m[:, :], compare_op=ALU.not_equal, fill=1.0, base=0,
                                   pattern=[[-1, P]], channel_multiplier=1).then_inc(const_ready, 1)
            pool.wait_ge(const_ready, 5)
            for step in PLAN:
                kind = step[0]
                if kind == "stats" or (kind == "out_proj" and step[1] == "cross"):
                    u = step[3]
                    pool.wait_ge(var_ready, stat_no[u] + 1)
                    pool.tensor_tensor(rstd[:, u % 4:u % 4 + 1], mv[:, u % 4, 1:2], half[:, 0:1],
                                       ALU.pow).then_inc(rstd_ready, 1)
                elif kind == "x_load" and step[1] in ("self", "cross"):
                    u = step[3]
                    if u == biased[0][3]:
                        pool.wait_ge(s_w["rest"], 128)
                    pool.wait_ge(x_loaded[u % 4], 16 * (u // 4 + 1))
                    pool.tensor_tensor(xb[:, u % 4, :], xb[:, u % 4, :], (bo_sb if step[1] == "self" else xbo_sb)[:, :],
                                       ALU.add).then_inc(x_biased, 1)
                elif kind == "lines_a":
                    pool.wait_ge(n2_ready, step[1] + 1)
                    pool.tensor_tensor(line_rn, line_n2, half[:, :], ALU.pow).then_inc(rn_ready, 1)
                elif kind == "scores" and step[1] in mask_no:
                    n = step[1]
                    off, _ = quad_cols(n)
                    for e in range(2):
                        s = 2 * n + e
                        pool.wait_ge(exp_done, s + 1)
                        d = probs[:, s % 4, :, off:off + P]
                        pool.affine_select(out=d, in_=d, compare_op=ALU.is_ge, fill=0.0, base=0,
                                           pattern=[[0, 2], [1, P]], channel_multiplier=-1).then_inc(mask_done, 1)
            pool.wait_ge(line_stored, 16 * TB)
            pool.memset(ones[:, :], 1.0).then_inc(const_ready, 1)

            def gather(i):
                if i >= 2:
                    pool.wait_ge(g_full, TG["xe", i - 2] + 1)
                pool.indirect_dma_start(
                    x_e[i % 2], None, xn_d, bass.IndirectOffsetOnAxis(idx_gather[:, i:i + 1], 0)
                ).then_inc(gathered[i % 2], 16)

            pool.wait_ge(g_free, TG["tops"] + 1)
            pool.wait_ge(picked, 4)
            for r in range(2):
                pool.wait_ge(xn_stored[r], 16 * TB // 2)
            for r in range(4):
                pool.wait_ge(x_stored[r], 16 * x_stores[r])
            gather(0)
            gather(1)
            for i in range(E // 2):
                if i + 2 < E // 2:
                    gather(i + 2)
                for e in range(2 * i, 2 * i + 2):
                    pool.wait_ge(y_ready, e + 1)
                    if e:
                        pool.wait_ge(scattered, 16 * e)
                    pool.indirect_dma_start(
                        out, bass.IndirectOffsetOnAxis(idx_scatter[:, e:e + 1], 0), y_e[2 * (i % 2) + e % 2][0:CAP, :], None,
                        compute_op=ALU.add).then_inc(scattered, 16)
            pool.wait_ge(scattered, 16 * E)

        @block.scalar
        def _(act):
            act.wait_ge(s_w["rest"], 128)
            act.activation(temp[:, 1:2], temp[:, 0:1], ACT.Exp).then_inc(temp_ready, 1)
            for step in PLAN:
                if step[0] == "scores":
                    n = step[1]
                    off, rows = quad_cols(n)
                    for e in range(2):
                        s = 2 * n + e
                        act.wait_ge(scores_full, s + 1)
                        if s >= 4:
                            act.wait_ge(pv_done, (s - 4) // 2 + 1)
                        act.activation(probs[0:rows, s % 4, :, off:], ps[s % 2][0:rows, :, off:], ACT.Exp,
                                       scale=LSCALE if QUADS[n][0] == "self" else 1.0).then_inc(exp_done, 1)
                elif step[0] == "weights":
                    if step[1] == 0:
                        act.wait_ge(pv_done, last_quad["self", NT - 1] + 1)
                    load_expert(act, step[1])
            act.wait_ge(pv_done, len(QUADS))
            for e in range(3, NSLOT):
                load_expert(act, e)
            act.wait_ge(sink_ready, 1)
            act.activation(affin[:, :, :], sink[:, :, :], ACT.Exp).then_inc(sink_act, 1)
            act.wait_ge(sink_ready, 2)
            act.activation(tmp16[:, 3, :], tmp16[:, 2, :], ACT.Ln).then_inc(sink_act, 1)
            act.wait_ge(g_free, TG["col_back"] + 1)
            act.activation(affin[:, :, :], sink[:, :, :], ACT.Exp).then_inc(sink_act, 1)
            for i in range(E // 2):
                act.wait_ge(h_turned, i + 1)
                if i >= 2:
                    act.wait_ge(g_full, TG["y", i - 2] + 1)
                act.activation(h_t[i % 2], ps[i % 2][:, :, :].rearrange("p a b -> p (a b)"),
                               ACT.Gelu_apprx_tanh).then_inc(gelu_done, 1)


        @block.vector
        def _(dve):
            steps = [0]

            def link(ins):
                steps[0] += 1
                ins.then_inc(dve_step, 1)
                dve.wait_ge(dve_step, steps[0])

            def full(step):
                dve.wait_ge(g_full, g_at(step) + 1)
                return pg[g_at(step) % 3]

            def block_stats(u):
                r = u % 4
                if u >= 4 and loads[u - 4][1] != "self":
                    dve.wait_ge(xn_ready, norm_no[u - 4] + 1)
                link(dve.bn_stats(bn[:, r, :], xb[:, r, :]))
                link(dve.bn_aggr(mv[:, r, :], bn[:, r, :]))
                dve.tensor_scalar(mv[:, r, 1:2], mv[:, r, 1:2], EPS, None, ALU.add).then_inc(var_ready, 1)

            def split(src, parts, n, g_count):
                link(dve.tensor_copy(parts[:, 0, 0:n], src))
                dve.tensor_tensor(rest[:, 0:n], src, parts[:, 0, 0:n], ALU.subtract).then_inc(g_free, 1)
                dve.wait_ge(g_free, g_count)
                link(dve.tensor_copy(parts[:, 1, 0:n], rest[:, 0:n]))
                dve.tensor_tensor(parts[:, 2, 0:n], rest[:, 0:n], parts[:, 1, 0:n],
                                  ALU.subtract).then_inc(parts_ready, 1)

            def parts_free(step):
                n = splits.index(step)
                if n >= 2:
                    dve.wait_ge(parts_stored[n % 2], 16 * (n // 2))
                    dve.wait_ge(parts_ready, n)
                return n % 2

            dve.memset(v_self[:, :, :], 0.0).then_inc(v_ones, 1)
            dve.memset(v_cross[:, :, :], 0.0).then_inc(v_ones, 1)
            dve.memset(k_cross[NS * DH:P, :, :], 1.0).then_inc(v_ones, 1)
            dve.wait_ge(v_ones, 3)
            for v in (v_self, v_cross):
                dve.memset(v[:, :, 0:H * VW].rearrange("p b (h v) -> p b h v", h=H)[:, :, :, DH],
                           1.0).then_inc(v_ones, 1)
            for step in PLAN:
                kind = step[0]
                if kind == "stats":
                    u = step[3]
                    dve.wait_ge(x_loaded[u % 4], 16 * (u // 4 + 1))
                    block_stats(u)
                elif kind == "norm":
                    u = step[3]
                    n = norm_no[u]
                    r = n % 2
                    dve.wait_ge(rstd_ready, stat_no[u] + 1)
                    if n >= 2:
                        dve.wait_ge(g_full, g_at(("x_turn", *norms[n - 2][1:])) + 1)
                        dve.wait_ge(xn_ready, n - 1)
                        stores = sum(1 for s in norms[r:n - 1:2] if s[1] == "cross")
                        if stores:
                            dve.wait_ge(xn_stored[r], 16 * stores)
                    dve.tensor_scalar(xn[:, r, :], xb[:, u % 4, :], mv[:, u % 4, 0:1], rstd[:, u % 4:u % 4 + 1],
                                      ALU.subtract, ALU.mult).then_inc(xn_ready, 1)
                elif kind == "carry":
                    if step[1] == 0:
                        link(dve.memset(xn_t[:, :, 0:1], 0.0))
                    else:
                        link(dve.tensor_copy(xn_t[:, :, 0], carry[:, :]))
                elif kind == "x_turn":
                    g = full(step)
                    c = 1 + (step[2] % BPT) * P
                    dve.tensor_copy(xn_t[:, :, c:c + P], g[:, 0:DK * P].rearrange("p (k n) -> p k n", k=DK)
                                    ).then_inc(g_free, 1)
                elif kind == "carry_out":
                    dve.wait_ge(g_free, g_at(("project", BPT * step[1] + BPT - 1)))
                    link(dve.tensor_copy(carry[:, :], xn_t[:, :, TILE]))
                elif kind == "project":
                    b = step[1]
                    if b == 0:
                        dve.wait_ge(s_w["rest"], 128)
                        dve.wait_ge(v_ones, 5)
                    g = full(step)
                    link(dve.tensor_tensor(v_self[:, b, 0:H * VW].rearrange("p (h v) -> p h v", h=H)[:, :, 0:DH],
                                           g[:, 256:512].rearrange("p (h d) -> p h d", h=H),
                                           bv_sb[:, :].rearrange("p (h d) -> p h d", h=H), ALU.add))
                    dve.tensor_copy(raw[:, b % BPT, :], g[:, 0:256]).then_inc(g_free, 1)
                elif kind == "lines_a":
                    j = step[1]
                    dve.wait_ge(g_free, g_at(("project", BPT * j + BPT - 1)) + 1)
                    if j:
                        dve.wait_ge(lines_split, j)
                    comp = raw.rearrange("p b (s q h i) -> p b s q h i", s=2, q=2, i=4)
                    lv = lines.rearrange("p (b s) h c -> p b s h c", s=2)
                    tv = lines_t.rearrange("p (b s) h c -> p b s h c", s=2)
                    for side, pairs in ((0, Q_PAIRS), (1, K_PAIRS)):
                        for c, (a, z) in enumerate(pairs):
                            dve.tensor_tensor(lv[:, :, side, :, c], comp[:, :, side, 0, :, a],
                                              comp[:, :, side, 1, :, z], ALU.mult)
                            last = dve.tensor_tensor(tv[:, :, side, :, c], comp[:, :, side, 0, :, z],
                                                     comp[:, :, side, 1, :, a], ALU.mult)
                    link(last)
                    flat = lines.rearrange("p s h c -> p (s h c)")
                    flat_t = lines_t.rearrange("p s h c -> p (s h c)")
                    link(dve.tensor_tensor(flat, flat, flat_t, ALU.subtract))
                    link(dve.tensor_tensor(flat_t, flat, flat, ALU.mult))
                    link(dve.reduce_sum(line_n2, lines_t.rearrange("p s h c -> p (s h) c"), AX_X))
                    dve.tensor_scalar(line_n2, line_n2, 1e-24, None, ALU.max).then_inc(n2_ready, 1)
                elif kind == "lines_b":
                    j = step[1]
                    dve.wait_ge(rn_ready, j + 1)
                    if j:
                        dve.wait_ge(g_full, g_at(("line_turn", BPT * j - 1)) + 1)
                    l3 = lines.rearrange("p s h c -> p (s h) c")
                    link(dve.tensor_tensor(l3, l3, line_rn.unsqueeze(2).broadcast_to((P, 8 * H, NC)), ALU.mult))
                    l2 = lines.rearrange("p s h c -> p s (h c)")
                    t2 = lines_t.rearrange("p s h c -> p s (h c)")
                    link(dve.tensor_copy(line_parts[:, :, 0, :], l2))
                    link(dve.tensor_tensor(t2, l2, line_parts[:, :, 0, :], ALU.subtract))
                    link(dve.tensor_copy(line_parts[:, :, 1, :], t2))
                    dve.tensor_tensor(line_parts[:, :, 2, :], t2, line_parts[:, :, 1, :],
                                      ALU.subtract).then_inc(lines_split, 1)
                elif kind == "line_turn":
                    b = step[1]
                    g = full(step)
                    if b:
                        dve.wait_ge(line_stored, 16 * b)
                    dve.tensor_copy(line_t[:, :, :], g[0:H * NC, 0:384].bitcast(BF16)
                                    .rearrange("p (a t) -> p a t", a=6)).then_inc(g_free, 1)
                elif kind == "ctx_k":
                    _, t, m = step
                    g = full(step)
                    r = parts_free(step)
                    n_keys = min(TILE, S - t * TILE)
                    split(g[:, 0:n_keys], parts_ctx[r], n_keys, g_at(step) + 1)
                elif kind == "ctx_v":
                    b = step[1]
                    if b == 0:
                        dve.wait_ge(v_ones, 5)
                    g = full(step)
                    nb = min(2, SB - b)
                    rows = min(P, S - b * P)
                    dve.tensor_copy(
                        v_cross[0:rows, b:b + nb, 0:H * VW].rearrange("p b (h v) -> p b h v", h=H)[:, :, :, 0:DH],
                        g[0:rows, 0:nb * D].rearrange("p (b h d) -> p b h d", b=nb, h=H)).then_inc(g_free, 1)
                elif kind == "o_evac":
                    _, which, j, gi, n = step
                    dve.wait_ge(pv_done, n + 1)
                    e = evac_no[which, j, gi]
                    if e >= 4:
                        users = [g_at(s) for s in PLAN if s[0] == "o_turn" and s[1] == evacs[e - 4][1]
                                 and s[2] // BPT == evacs[e - 4][2]]
                    else:
                        users = ctx_users
                    dve.wait_ge(g_full, max(users) + 1)
                    dve.tensor_copy(o_sb[:, gi, :], po[:, :]).then_inc(o_free, 1)
                elif kind == "o_turn":
                    g = full(step)
                    gv = g[:, :].rearrange("p (h r) -> p h r", r=32)
                    link(dve.reciprocal(rsum[:, :], gv[:, :, DH]))
                    dve.tensor_tensor(attn[:, :].rearrange("p (h d) -> p h d", h=H), gv[:, :, 0:DH],
                                      rsum[:, :].unsqueeze(2).broadcast_to((P, H, DH)), ALU.mult).then_inc(g_free, 1)
                elif kind == "a_turn":
                    g = full(step)
                    dve.tensor_copy(attn_t[:, :, :], g[:, 0:DK * P].rearrange("p (k n) -> p k n", k=DK)
                                    ).then_inc(g_free, 1)
                elif kind == "out_proj":
                    _, which, b, u = step
                    g = full(step)
                    dve.wait_ge(x_biased, bias_no[u] + 1)
                    dve.tensor_tensor(xb[:, u % 4, :], g[:, 0:D], xb[:, u % 4, :], ALU.add).then_inc(g_free, 1)
                    if which == "cross":
                        dve.wait_ge(g_free, g_at(step) + 1)
                        block_stats(u)
                elif kind == "x_query":
                    g = full(step)
                    r = parts_free(step)
                    if step[1] == 0:
                        dve.wait_ge(g_full, g_at(("project", TB - 1)) + 1)
                    split(g[:, :], parts_q[r], TILE, g_at(step) + 1)
                elif kind == "max":
                    _, j, b, h, c = step
                    g = full(step)
                    n_keys = min(TILE, S - c * TILE)
                    dve.reduce_max(mx[:, b % 2, h, c:c + 1], g[:, 0:n_keys], AX_X).then_inc(g_free, 1)
                elif kind == "shift":
                    _, j, b = step
                    if b:
                        dve.wait_ge(g_full, g_at(("shift_turn", (b - 1) // BPT, b - 1)) + 1)
                    dve.wait_ge(g_free, g_at(("max", j, b, H - 1, ST - 1)) + 1)
                    f0, f1 = shift_f[:, 0, :], shift_f[:, 1, :]
                    link(dve.reduce_max(f0, mx[:, b % 2, :, :], AX_X))
                    link(dve.tensor_scalar(f1, f0, -1.0, None, ALU.mult))
                    link(dve.tensor_copy(shift_parts[:, 0, :], f1))
                    link(dve.tensor_tensor(f0, f1, shift_parts[:, 0, :], ALU.subtract))
                    link(dve.tensor_copy(shift_parts[:, 1, :], f0))
                    dve.tensor_tensor(shift_parts[:, 2, :], f0, shift_parts[:, 1, :],
                                      ALU.subtract).then_inc(shift_split, 1)
                elif kind == "shift_turn":
                    _, j, b = step
                    g = full(step)
                    if b % BPT == 0 and j:
                        dve.wait_ge(shift_stored, 16 * j)
                    dve.tensor_copy(shift_t[:, (b % BPT) * P:(b % BPT + 1) * P],
                                    g[0:3 * H, 0:P // 2].bitcast(BF16)).then_inc(g_free, 1)
                elif kind == "gate":
                    b = step[1]
                    g = full(step)
                    dve.tensor_copy(logits[:, b, :], g[:, 0:E]).then_inc(g_free, 1)

            def col_view(ap):
                return ap.rearrange("p b e -> p e b")

            def over_experts(v):
                return v.unsqueeze(2).broadcast_to((P, TB, E))

            def over_blocks(v):
                return v.unsqueeze(1).broadcast_to((P, TB, E))

            row, col = tmp16[:, 0, :], tmp16[:, 1, :]
            dve.wait_ge(const_ready, 6)
            dve.wait_ge(temp_ready, 1)
            link(dve.reciprocal(temp[:, 0:1], temp[:, 1:2]))
            dve.wait_ge(g_free, NG)
            link(dve.tensor_scalar(sink[:, :, :], logits[:, :, :], temp[:, 0:1], None, ALU.mult))
            link(dve.reduce_max(row, sink[:, :, :], AX_X))
            dve.tensor_tensor(sink[:, :, :], sink[:, :, :], over_experts(row), ALU.subtract).then_inc(sink_ready, 1)
            dve.wait_ge(sink_act, 1)
            link(dve.reduce_sum(row, affin[:, :, :], AX_X))
            dve.tensor_copy(tmp16[:, 2, :], row).then_inc(sink_ready, 1)
            dve.wait_ge(sink_act, 2)
            link(dve.tensor_tensor(sink[:, :, :], sink[:, :, :], over_experts(tmp16[:, 3, :]), ALU.subtract))
            dve.reduce_max(col, col_view(sink[:, :, :]), AX_X).then_inc(router_pe, 1)
            g = tail_full(dve, "col_turn")
            dve.reduce_max(turned[:, 1, 0:1], g[0:E, 0:P], AX_X).then_inc(g_free, 1)
            dve.wait_ge(g_free, TG["col_turn"] + 1)
            dve.tensor_scalar(turned[:, 0, :], ones[0:E, :], turned[:, 1, 0:1], None, ALU.mult).then_inc(router_pe, 1)
            g = tail_full(dve, "col_back")
            dve.tensor_tensor(sink[:, :, :], sink[:, :, :], over_blocks(g[:, 0:E]), ALU.subtract).then_inc(g_free, 1)
            dve.wait_ge(sink_act, 3)
            for it in range(SINK_ITERS):
                if it:
                    link(dve.reduce_sum(row, affin[:, :, :], AX_X))
                    link(dve.reciprocal(row, row))
                    dve.tensor_tensor(affin[:, :, :], affin[:, :, :], over_experts(row),
                                      ALU.mult).then_inc(router_pe, 1)
                g = tail_full(dve, ("col_sum", it))
                dve.reduce_sum(col, g[:, 0:TB * E].rearrange("p (b e) -> p e b", b=TB), AX_X).then_inc(g_free, 1)
                dve.wait_ge(g_free, TG["col_sum", it] + 1)
                link(dve.reciprocal(col, col))
                last = dve.tensor_tensor(affin[:, :, :], affin[:, :, :], over_blocks(col), ALU.mult)
                if it < SINK_ITERS - 1:
                    link(last)
                else:
                    last.then_inc(router_pe, 1)
            for c in range(4):
                g = tail_full(dve, ("aff", c))
                dve.tensor_copy(affinity[:, c * TILE:(c + 1) * TILE], g[0:E, :]).then_inc(g_free, 1)
            dve.wait_ge(g_free, TG["aff", 3] + 1)
            idx = tops[:, 1, :].bitcast(U32)
            for r in range(CAP // 8):
                vals = tops[:, 0, 8 * r:8 * r + 8]
                link(dve.max(vals, affinity))
                link(dve.max_index(idx[:, 8 * r:8 * r + 8], vals, affinity))
                if r < CAP // 8 - 1:
                    link(dve.match_replace(out=affinity, in_to_replace=vals, in_values=affinity, imm_value=-1.0))
            dve.tensor_copy(tops[:, 2, :], idx).then_inc(router_pe, 1)
            g = tail_full(dve, "tops")
            for e in range(2):
                for dst, c0 in ((gates, 0), (idx_gather, E)):
                    dve.tensor_copy(dst[CAP * e:CAP * (e + 1), :],
                                    g[0:CAP, c0:c0 + E].rearrange("p (i e) -> p e i", e=2)[:, e, :]).then_inc(picked, 1)
            dve.tensor_copy(idx_scatter[:, :], g[0:CAP, E:2 * E]).then_inc(g_free, 1)
            dve.wait_ge(picked, 4)

            def expert_in(i):
                g = tail_full(dve, ("xe", i))
                dve.tensor_copy(x_et[i % 2], g[:, 0:DK * P].rearrange("p (k n) -> p k n", k=DK)).then_inc(g_free, 1)

            def hidden(i):
                dve.wait_ge(bias_loaded[i % 2], 64 * (i // 2 + 1))
                if i >= 2:
                    dve.wait_ge(h_turned, i - 1)
                for f in range(2):
                    g = tail_full(dve, ("h", i, f))
                    dve.tensor_tensor(h_sb[i % 2][:, f * TILE:(f + 1) * TILE], g[:, :],
                                      b1_sb[i % 2][:, f * TILE:(f + 1) * TILE], ALU.add).then_inc(g_free, 1)

            def expert_out(i):
                g = tail_full(dve, ("y", i))
                if i >= 1:
                    dve.wait_ge(y_ready, 2 * i)
                dve.tensor_tensor(rest[:, 0:D], g[:, 0:D], b2_sb[i % 2], ALU.add).then_inc(g_free, 1)
                dve.wait_ge(g_free, TG["y", i] + 1)
                for e in range(2):
                    if i >= 2:
                        dve.wait_ge(scattered, 16 * (2 * (i - 2) + e + 1))
                    dve.tensor_scalar(y_e[2 * (i % 2) + e][0:CAP, :], rest[CAP * e:CAP * (e + 1), 0:D],
                                      gates[CAP * e:CAP * (e + 1), i:i + 1], None, ALU.mult).then_inc(y_ready, 1)

            expert_in(0)
            hidden(0)
            for i in range(E // 2):
                if i + 1 < E // 2:
                    expert_in(i + 1)
                    hidden(i + 1)
                expert_out(i)

        @block.tensor
        def _(pe):
            def bank(step):
                n = g_at(step)
                if n >= 3:
                    pe.wait_ge(g_free, n - 2)
                return pg[n % 3]

            def after(step):
                pe.wait_ge(g_free, g_at(step) + 1)

            def scores(n):
                kind, j, g, i, _ = QUADS[n]
                off, rows = quad_cols(n)
                if kind == "self" and g == 0 and i == 0:
                    pe.wait_ge(lines_loaded[j], 16 * 24)
                if kind == "cross" and g == 0 and i == 0:
                    pe.wait_ge(shift_loaded[j], 16)
                for e in range(2):
                    s = 2 * n + e
                    if s >= 2:
                        pe.wait_ge(exp_done, s - 1)
                    for a in range(2):
                        h = 4 * g + 2 * e + a
                        if kind == "self":
                            r = 64 * a
                            lhs = k_line[r:r + NS * NC, h // 2, i * P:(i + 1) * P]
                            rhs = q_line[j % 2][r:r + NS * NC, h // 2, off:]
                        else:
                            lhs = k_cross[0:NS * DH + 3, h, i * P:i * P + rows]
                            rhs = q_cross[j % 2][0:NS * DH + 3, h, :]
                        mm = pe.matmul(ps[s % 2][0:rows, a, off:], lhs, rhs, start=True, stop=True)
                    mm.then_inc(scores_full, 1)

            def values(n):
                kind, j, g, i, end = QUADS[n]
                off, rows = quad_cols(n)
                if n in mask_no:
                    pe.wait_ge(mask_done, 2 * mask_no[n] + 2)
                else:
                    pe.wait_ge(exp_done, 2 * n + 2)
                if i == 0:
                    e = evac_no[kind, j, g]
                    if e:
                        pe.wait_ge(o_free, e)
                v = v_self if kind == "self" else v_cross
                for a in range(4):
                    h = 4 * g + a
                    s = 2 * n + a // 2
                    mm = pe.matmul(po[32 * a:32 * a + 32, off:], v[0:rows, i, h * VW:h * VW + 32],
                                   probs[0:rows, s % 4, a % 2, off:], start=(i == 0),
                                   stop=end or (kind == "self" and i >= BPT * j), skip_group_check=off > 0)
                mm.then_inc(pv_done, 1)

            pe.wait_ge(const_ready, 5)
            for step in PLAN:
                kind = step[0]
                if kind == "scores":
                    scores(step[1])
                elif kind == "pv":
                    values(step[1])
                if step not in G_USE:
                    continue
                g = bank(step)
                if kind == "ctx_k":
                    _, t, m = step
                    if step == ("ctx_k", 0, 0):
                        pe.wait_ge(s_w["ctx"], 16)
                        pe.wait_ge(s_w["xk"], 16)
                    n_keys = min(TILE, S - t * TILE)
                    for k in range(DK):
                        mm = pe.matmul(g[:, 0:n_keys], wxk_sb[:, k, m * P:(m + 1) * P],
                                       ctx_sb[:, k, t * TILE:t * TILE + n_keys], start=(k == 0), stop=(k == DK - 1))
                elif kind == "ctx_v":
                    b0 = step[1]
                    if b0 == 0:
                        pe.wait_ge(s_w["xv"], 16)
                    for b in range(b0, min(b0 + 2, SB)):
                        rows = min(P, S - b * P)
                        for k in range(DK):
                            mm = pe.matmul(g[0:rows, (b - b0) * D:(b - b0 + 1) * D], ctx_sb[:, k, b * P:b * P + rows],
                                           wxv_sb[:, k, :], start=(k == 0), stop=(k == DK - 1))
                elif kind == "x_turn":
                    u = step[3]
                    pe.wait_ge(xn_ready, norm_no[u] + 1)
                    for k in range(DK):
                        mm = pe.transpose(g[:, k * P:(k + 1) * P], xn[:, norm_no[u] % 2, k * P:(k + 1) * P], ident[:, :])
                elif kind == "project":
                    b = step[1]
                    if b == 0:
                        pe.wait_ge(s_w["self"], 16)
                        pe.wait_ge(dve_step, 1)
                    pe.wait_ge(g_free, g_at([s for s in PLAN if s[:3] == ("x_turn", "prep", b)][0]) + 1)
                    c = (b % BPT) * P
                    for k in range(DK):
                        pe.matmul(g[:, :], xn_t[:, k, c + 1:c + 1 + P], wself_sb[:, k, 0:512], start=(k == 0), stop=False)
                    for k in range(DK):
                        mm = pe.matmul(g[:, 0:P], xn_t[:, k, c:c + P], wself_sb[:, k, 512:640], start=False,
                                       stop=(k == DK - 1))
                elif kind == "line_turn":
                    b = step[1]
                    pe.wait_ge(lines_split, b // BPT + 1)
                    gb = g[:, :].bitcast(BF16)
                    for a in range(6):
                        mm = pe.transpose(gb[0:H * NC, a * P:(a + 1) * P],
                                          line_parts[:, 2 * (b % BPT) + a // 3, a % 3, :], identb[:, :])
                elif kind == "o_turn":
                    _, which, b, u = step
                    pe.wait_ge(o_free, evac_no[which, b // BPT, 3] + 1)
                    c = (b % BPT) * P
                    for gi in range(4):
                        mm = pe.transpose(g[:, gi * P:(gi + 1) * P], o_sb[:, gi, c:c + P], ident[:, :])
                elif kind == "a_turn":
                    after(("o_turn", *step[1:]))
                    for k in range(DK):
                        mm = pe.transpose(g[:, k * P:(k + 1) * P], attn[:, k * P:(k + 1) * P], ident[:, :])
                elif kind == "out_proj":
                    if step == joins[0]:
                        pe.wait_ge(s_w["rest"], 128)
                    after(("a_turn", *step[1:]))
                    for k in range(DK):
                        mm = pe.matmul(g[:, 0:D], attn_t[:, k, :], (wo_sb if step[1] == "self" else wxo_sb)[:, k, :],
                                       start=(k == 0), stop=(k == DK - 1))
                elif kind == "x_query":
                    _, j, m = step
                    after([s for s in PLAN if s[:3] == ("x_turn", "query", BPT * j + BPT - 1)][0])
                    for k in range(DK):
                        mm = pe.matmul(g[:, :], wxq_sb[:, k, m * P:(m + 1) * P], xn_t[:, k, 1:1 + TILE],
                                       start=(k == 0), stop=(k == DK - 1))
                elif kind == "max":
                    _, j, b, h, c = step
                    if b % BPT == 0 and h == 0 and c == 0:
                        pe.wait_ge(query_loaded[j], 16 * NS)
                        pe.wait_ge(ctx_loaded, 16 * NS * ST)
                    n_keys = min(TILE, S - c * TILE)
                    q = (b % BPT) * P
                    mm = pe.matmul(g[:, 0:n_keys], q_cross[j % 2][0:NS * DH, h, q:q + P],
                                   k_cross[0:NS * DH, h, c * TILE:c * TILE + n_keys], start=True, stop=True)
                elif kind == "shift_turn":
                    b = step[2]
                    pe.wait_ge(shift_split, b + 1)
                    mm = pe.transpose(g[:, :].bitcast(BF16)[0:3 * H, 0:P],
                                      shift_parts[:, :, :].rearrange("p q h -> p (q h)"), identb[:, :])
                elif kind == "gate":
                    b = step[1]
                    after([s for s in PLAN if s[:3] == ("x_turn", "cross", b)][0])
                    c = 1 + (b % BPT) * P
                    for k in range(DK):
                        mm = pe.matmul(g[:, 0:E], xn_t[:, k, c:c + P], gate_sb[:, k, :],
                                       start=(k == 0), stop=(k == DK - 1))
                mm.then_inc(g_full, 1)

            g = tail_bank(pe, "col_turn")
            pe.wait_ge(router_pe, 1)
            pe.transpose(g[0:E, 0:P], tmp16[:, 1, :], ident[:, :]).then_inc(g_full, 1)
            g = tail_bank(pe, "col_back")
            pe.wait_ge(router_pe, 2)
            pe.matmul(g[:, 0:E], turned[:, 0, :], ident[0:E, 0:E], start=True, stop=True).then_inc(g_full, 1)
            pe.wait_ge(const_ready, 6)
            for it in range(SINK_ITERS):
                g = tail_bank(pe, ("col_sum", it))
                if it:
                    pe.wait_ge(router_pe, 2 + it)
                else:
                    pe.wait_ge(sink_act, 3)
                pe.matmul(g[:, 0:TB * E], ones[:, :], affin.rearrange("p b e -> p (b e)"), start=True,
                          stop=True).then_inc(g_full, 1)
            pe.wait_ge(router_pe, 2 + SINK_ITERS)
            for c in range(4):
                g = tail_bank(pe, ("aff", c))
                for b in range(4):
                    mm = pe.transpose(g[0:E, b * P:(b + 1) * P], affin[:, 4 * c + b, :], ident[:, :])
                mm.then_inc(g_full, 1)
            g = tail_bank(pe, "tops")
            pe.wait_ge(router_pe, 3 + SINK_ITERS)
            pe.transpose(g[0:CAP, 0:E], tops[:, 0, :], ident[0:E, 0:E])
            pe.transpose(g[0:CAP, E:2 * E], tops[:, 2, :], ident[0:E, 0:E]).then_inc(g_full, 1)

            def expert_in(i):
                g = tail_bank(pe, ("xe", i))
                pe.wait_ge(gathered[i % 2], 16 * (i // 2 + 1))
                for k in range(DK):
                    mm = pe.transpose(g[:, k * P:(k + 1) * P], x_e[i % 2][:, k * P:(k + 1) * P], ident[:, :])
                mm.then_inc(g_full, 1)

            def hidden(i):
                for e in range(2):
                    n = 2 * i + e
                    pe.wait_ge(slot_loaded[n % NSLOT], 32 * (n // NSLOT + 1))
                pe.wait_ge(g_free, TG["xe", i] + 1)
                for f in range(2):
                    g = tail_bank(pe, ("h", i, f))
                    for k in range(DK):
                        for e in range(2):
                            w = slots[(2 * i + e) % NSLOT][:, 0:2048].rearrange("p (k n) -> p k n", k=DK)
                            mm = pe.matmul(g[CAP * e:CAP * (e + 1), :], x_et[i % 2][:, k, CAP * e:CAP * (e + 1)],
                                           w[:, k, f * TILE:(f + 1) * TILE], start=(k == 0), stop=(k == DK - 1))
                    mm.then_inc(g_full, 1)

            def turn_hidden(i):
                pe.wait_ge(g_free, TG["h", i, 1] + 1)
                if i >= 2:
                    pe.wait_ge(gelu_done, i - 1)
                else:
                    pe.wait_ge(exp_done, 2 * len(QUADS))
                pt = ps[i % 2][:, :, :].rearrange("p a b -> p (a b)")
                for f in range(8):
                    mm = pe.transpose(pt[:, f * P:(f + 1) * P], h_sb[i % 2][:, f * P:(f + 1) * P], ident[:, :])
                mm.then_inc(h_turned, 1)

            def expert_out(i):
                g = tail_bank(pe, ("y", i))
                pe.wait_ge(gelu_done, i + 1)
                for f in range(8):
                    for e in range(2):
                        w = slots[(2 * i + e) % NSLOT][:, 2048:4096].rearrange("p (k n) -> p k n", k=8)
                        mm = pe.matmul(g[CAP * e:CAP * (e + 1), 0:D],
                                       h_t[i % 2][:, f * P + CAP * e:f * P + CAP * (e + 1)], w[:, f, :],
                                       start=(f == 0), stop=(f == 7))
                mm.then_inc(g_full, 1)

            expert_in(0)
            hidden(0)
            for i in range(E // 2):
                turn_hidden(i)
                if i + 1 < E // 2:
                    expert_in(i + 1)
                    hidden(i + 1)
                expert_out(i)


def kernel(**inputs):
    import numpy as np
    import concourse.bacc as bacc
    from concourse.bass_utils import run_bass_kernel_spmd

    def turned(name):
        return np.ascontiguousarray(np.asarray(inputs[name]).T)

    def array(name):
        return np.ascontiguousarray(np.asarray(inputs[name]))

    w1q, w2q = turned("L0_attn_W1_q"), turned("L0_attn_W2_q")
    layout = {
        "x": array("x").reshape(T, D),
        "ctx_t": np.ascontiguousarray(array("ctx_1024").reshape(S, D).T),
        "w_self": np.concatenate([w1q[:D], w2q[:D], turned("L0_attn_W1_k"), turned("L0_attn_W2_k"),
                                  turned("L0_attn_Wv"), w1q[D:], w2q[D:]], axis=1),
        "w_o": turned("L0_attn_Wo"),
        "w_xq": turned("L0_xattn_Wq"),
        "w_xk": turned("L0_xattn_Wk"),
        "w_xv": turned("L0_xattn_Wv"),
        "w_xo": turned("L0_xattn_Wo"),
        "bv": array("L0_attn_bv"),
        "bo": array("L0_attn_bo"),
        "xbo": array("L0_xattn_bo"),
        "gate_t": turned("L0_ffn_gate_query"),
        "log_temp": array("L0_ffn_log_temp").reshape(1),
        "w1": array("L0_ffn_w1"),
        "b1": array("L0_ffn_b1"),
        "w2": array("L0_ffn_w2"),
        "b2": array("L0_ffn_b2"),
    }
    nc = bacc.Bacc("TRN2", target_bir_lowering=False, num_devices=1)
    args = [nc.dram_tensor(f"in_{n}", a.shape, mybir.dt.from_np(a.dtype), kind="ExternalInput").ap()
            for n, a in layout.items()]
    out = nc.dram_tensor("out", (T, D), F32, kind="ExternalOutput").ap()
    decoder_layer(nc, *args, out)
    r = run_bass_kernel_spmd(nc, [{f"in_{n}": a for n, a in layout.items()}], core_ids=[0])
    return r.results[0]["out"].reshape(1, T, D)
```

```python
from contextlib import ExitStack

import concourse.bass as bass
import numpy as np
from concourse import mybir

F32 = mybir.dt.float32
BF16 = mybir.dt.bfloat16
U32 = mybir.dt.uint32
I32 = mybir.dt.int32
ALU = mybir.AluOpType
ACT = mybir.ActivationFunctionType
AX_X = mybir.AxisListType.X

P = 128
T = 2048
D = 256
DK = D // P
S = 1601
H = 16
DH = D // H
VW = DH + 1
VB = H * VW + (32 - VW)
VP = 288
NC = 6
TB = T // P
TILE = 512
NT = T // TILE
BPT = TILE // P
SB = -(-S // P)
SP = 1604
ST = -(-S // TILE)
E = 16
CAP = 64
FF = 1024
NSLOT = 8
NCH = P // E
CHUNK = T // NCH
NBIAS = 3
EPS = 1e-5
SINK_ITERS = 6
LSCALE = 6.0 ** -0.5
BF16_ONES = float(np.array([0x3F803F80], np.uint32).view(np.float32)[0])
Q_PAIRS = [(0, 1), (0, 2), (0, 3), (1, 2), (1, 3), (2, 3)]
K_PAIRS = [(2, 3), (3, 1), (1, 2), (0, 3), (2, 0), (0, 1)]
Q_SLOTS = (0, 1, 0, 1, 2, 0)
K_SLOTS = (0, 0, 1, 1, 0, 2)
NS = len(Q_SLOTS)


def weave(steps, fill):
    out, done = [], 0
    for i, s in enumerate(steps):
        upto = len(fill) * (i + 1) // len(steps)
        out += [s] + fill[done:upto]
        done = upto
    return [s for s in out if s[0] != "gap"]


def build_plan():
    quads, w = [], [0]

    def attend(kind, j):
        out = []
        for g in range(4):
            blocks = BPT * (j + 1) if kind == "self" else SB
            for i in range(blocks):
                n = len(quads)
                quads.append((kind, j, g, i, i == blocks - 1))
                out += [[("scores", n, 0)], [("scores", n, 1)]]
                if n:
                    k, jj, gg, _, end = quads[n - 1]
                    out.append([("pv", n - 1)] + ([("o_evac", k, jj, gg, n - 1)] if end else []))
        return out

    def load_x(kind, j):
        use = []
        for b in range(BPT * j, BPT * j + BPT):
            use.append((b, w[0]))
            w[0] += 1
        return use

    def norm_steps(use, kind):
        s = [("x_load", kind, b, u) for b, u in use]
        s += [("stats", kind, b, u) for b, u in use]
        return s

    def prep(j):
        use = load_x("prep", j)
        s = norm_steps(use, "prep") + [("carry", j)]
        for n, (b, u) in enumerate(use):
            s += [("norm", "prep", b, u), ("x_turn", "prep", b, u)]
            if n:
                s += [("project", use[n - 1][0])]
        s += [("project", use[-1][0]), ("carry_out", j)]
        turns = [("lines", j)] + [("gap",)] * 10
        for b, _ in use:
            turns += [("line_turn", b), ("gap",)]
        return s, turns + [("line_load", j)]

    def join(kind, j):
        use = load_x(kind, j)
        s = [("x_load", kind, b, u) for b, u in use]
        for n in range(len(use) + (4 if kind == "cross" else 1)):
            if 0 <= n - 1 < len(use):
                s += [("a_turn", kind, *use[n - 1])]
            if n < len(use):
                s += [("o_turn", kind, *use[n])]
            if 0 <= n - 1 < len(use):
                s += [("out_proj", kind, *use[n - 1])]
            if kind == "cross" and 0 <= n - 2 < len(use):
                s += [("norm", "cross", *use[n - 2]), ("x_turn", "cross", *use[n - 2])]
            if kind == "cross" and 0 <= n - 3 < len(use):
                s += [("gate", use[n - 3][0])]
        return s

    def query(j):
        use = load_x("query", j)
        head = norm_steps(use, "query") + [("gap",)]
        for b, u in use:
            head += [("norm", "query", b, u), ("x_turn", "query", b, u)]
        head += [("x_query", j, m) for m in range(DK)]
        body = []
        for b, _ in use:
            m = [("max", j, b, h, c) for h in range(H) for c in range(ST)]
            if b > BPT * j:
                m[4:4] = [("shift", j, b - 1)]
                m[12:12] = [("shift_turn", j, b - 1)]
            body += m
        b = BPT * j + BPT - 1
        end = [("shift", j, b), ("gap",), ("gap",), ("shift_turn", j, b), ("shift_load", j)] + [("gap",)] * 10
        return head, body, end

    ctx = []
    for t in range(ST):
        ctx += [("ctx_k", t, 0), ("ctx_k", t, 1)]
        ctx += [("ctx_v", b) for b in range(BPT * t, min(BPT * t + BPT, SB), 2)]
        ctx += [("ctx_load", t)]
    p0, turns = prep(0)
    at = p0.index(("carry", 0))
    third = len(ctx) // 3
    plan = p0[:at] + weave(p0[at:], ctx[:third])

    def run(steps, fill):
        for s in weave([("quad", s) for s in steps], fill):
            if s[0] == "quad":
                plan.extend(s[1])
            else:
                plan.append(s)

    def mix(head, steps, fill):
        n = min(len(fill), len(steps))
        out = []
        for a, z in zip(steps[:n], fill[:n]):
            out += [a, z]
        return head + out + steps[n:] + fill[n:]

    def behind_lines(turns, head):
        return turns[:1] + head[:BPT] + turns[1:] + head[BPT:]

    def late(steps, head):
        at = len(steps) - 3 * len(head)
        out = steps[:at]
        for i, h in enumerate(head):
            out += [h] + steps[at + 3 * i:at + 3 * i + 3]
        return out

    p1, turns1 = prep(1)
    plan += turns[:1] + p1[:BPT] + weave(turns[11:], ctx[third:2 * third])
    plan += weave(p1[BPT:], ctx[2 * third:])
    p2, turns2 = prep(2)
    run(attend("self", 0), behind_lines(turns1, p2))
    sa1, sa2, sa3 = (attend("self", j) for j in (1, 2, 3))
    run(sa1[:21], [("gap",)] * 2 + join("self", 0))
    p3, turns3 = prep(3)
    run(sa1[21:], behind_lines(turns2, p3))
    run(sa2[:33], [("gap",)] * 2 + join("self", 1))
    head, body, end = query(0)
    fill = behind_lines(turns3, head) + [("query_load", 0)] + [("gap",)] * 16
    early = (len(body) + 3 * len(fill)) // 6
    run(sa2[33:], fill + body[:early])
    jn = [("gap",)] * 4 + join("self", 2)
    later = body[early + 40:] + end
    run(sa3[:45], mix([], jn, body[early:early + 40]))
    head, body, next_end = query(1)
    run(sa3[45:], late(later, head))
    for j in range(NT - 1):
        xa = attend("cross", j)
        jn = join("self", 3) if j == 0 else join("cross", j - 1)
        fill = mix(jn[:BPT] + [("query_load", j + 1), ("gap",), ("gap",)], jn[BPT:], [("gap",)] * 8 + body)
        fill += next_end
        if j == 0:
            for e in range(3):
                fill.insert(len(fill) // 2 + 30 * e, ("weights", e))
        if j + 2 < NT:
            head, body, next_end = query(j + 2)
            fill = late(fill, head)
        run(xa, fill)
    xa = attend("cross", NT - 1)
    run(xa[:36], [("gap",)] * 4 + join("cross", NT - 2))
    jn = join("cross", NT - 1)
    run(xa[36:], jn[:BPT])
    jn = jn[BPT:]
    plan += [("pv", len(quads) - 1), ("o_evac", "cross", NT - 1, 3, len(quads) - 1)]
    plan += jn
    g_use = {}
    G_STEPS = ("ctx_k", "ctx_v", "x_turn", "project", "line_turn", "o_turn", "a_turn", "out_proj", "x_query", "max",
               "shift_turn", "gate")
    for s in plan:
        if s[0] in G_STEPS:
            assert s not in g_use
            g_use[s] = len(g_use)
    return plan, quads, g_use


def decoder_layer(nc, x, ctx_t, w_self, w_o, w_xq, w_xk, w_xv, w_xo, bv, bo, xbo, gate_t, log_temp, w1, b1, w2, b2, out):
    PLAN, QUADS, G_USE = build_plan()
    n_plan = len(PLAN)
    where = {s: n for n, s in enumerate(PLAN)}

    line_d = nc.dram_tensor("line_d", (2, 3, H * NC, T), BF16, kind="Internal").ap()
    xk_d = nc.dram_tensor("xk_d", (3, D, SP), BF16, kind="Internal").ap()
    xq_d = nc.dram_tensor("xq_d", (3, D, T), BF16, kind="Internal").ap()
    shift_d = nc.dram_tensor("shift_d", (3, H, T), BF16, kind="Internal").ap()
    x1_d = nc.dram_tensor("x1_d", (T, D), F32, kind="Internal").ap()
    xn_d = nc.dram_tensor("xn_d", (T, D), F32, kind="Internal").ap()
    affin_d = nc.dram_tensor("affin_d", (T, E), F32, kind="Internal").ap()

    ctx = ExitStack()
    with ctx:
        def sb(name, shape, dt=F32):
            return ctx.enter_context(nc.sbuf_tensor(name, shape, dt))

        def sem(name):
            return ctx.enter_context(nc.semaphore(name))

        self_region = sb("self_region", [P, 16896])
        k_line = self_region[:, 0:8192].bitcast(BF16).rearrange("p (a t) -> p a t", a=8)
        v_self = self_region[:, 8192:8192 + TB * VP].rearrange("p (b v) -> p b v", b=TB)
        q_line = [self_region[:, 12800 + 2048 * r:14848 + 2048 * r].bitcast(BF16).rearrange("p (a t) -> p a t", a=8)
                  for r in range(2)]
        cross_region = sb("cross_region", [P, H * SP // 2 + SB * VP])
        k_cross = cross_region[:, 0:H * SP // 2].bitcast(BF16).rearrange("p (h s) -> p h s", h=H)
        v_cross = cross_region[:, H * SP // 2:].rearrange("p (b v) -> p b v", b=SB)
        probs = sb("probs", [P, 4, 2, TILE])
        probs_flat = probs[:, :, :, :].rearrange("p a b c -> p (a b c)")
        ctx_sb = probs_flat[:, 0:DK * S].rearrange("p (k s) -> p k s", k=DK)
        even_region = sb("even_region", [P, 4096])
        raw = even_region[:, 0:1024].rearrange("p (b n) -> p b n", b=BPT)
        lines = even_region[:, 1024:1792].rearrange("p (s h c) -> p s h c", s=8, h=H)
        lines_t = even_region[:, 1792:2560].rearrange("p (s h c) -> p s h c", s=8, h=H)
        line_parts = even_region[:, 2560:3712].bitcast(BF16).rearrange("p (s q n) -> p s q n", s=8, q=3)
        line_n2 = even_region[:, 3712:3840]
        line_rn = even_region[:, 3840:3968]
        q_cross = [even_region[:, 0:4096].bitcast(BF16).rearrange("p (h t) -> p h t", h=H),
                   self_region[:, 0:4096].bitcast(BF16).rearrange("p (h t) -> p h t", h=H)]
        slots = [self_region[:, 4096 * (s + 1):4096 * (s + 2)] for s in range(3)]
        slots += [cross_region[:, 4096 * s:4096 * (s + 1)] for s in range(4)]
        slots += [probs_flat]

        o_region = sb("o_region", [P, 4 * TILE])
        o_sb = o_region[:, :].rearrange("p (g t) -> p g t", g=4)
        wxk_sb = o_region[:, 0:512].rearrange("p (k n) -> p k n", k=DK)
        wxv_sb = o_region[:, 512:1024].rearrange("p (k n) -> p k n", k=DK)
        xn_t = sb("xn_t", [P, DK, TILE + 1])
        carry = sb("carry", [P, DK])
        xb = sb("xb", [P, 4, D])
        xn = sb("xn", [P, 2, D])
        bn = sb("bn", [P, 4, 6])
        mv = sb("mv", [P, 4, 2])
        rstd = sb("rstd", [P, 4])
        attn = sb("attn", [P, D])
        rsum = sb("rsum", [P, H])
        attn_t = sb("attn_t", [P, DK, P])
        late_region = sb("late_region", [P, 384])
        line_t = late_region[0:H * NC, :].bitcast(BF16).rearrange("p (a t) -> p a t", a=6)
        wself_sb = sb("wself_sb", [P, DK, 640])
        parts_a = sb("parts_a", [P, 3, TILE], BF16)
        rest = sb("rest", [P, TILE])
        shift_parts = sb("shift_parts", [P, 3, H], BF16)
        shift_t = sb("shift_t", [3 * H, TILE], BF16)
        shift_f = sb("shift_f", [P, 2, H])
        mx = sb("mx", [P, 2, H, ST])
        wo_sb = sb("wo_sb", [P, DK, D])
        wxq_sb = sb("wxq_sb", [P, DK, D])
        wxo_sb = sb("wxo_sb", [P, DK, D])
        gate_sb = sb("gate_sb", [P, DK, E])
        bv_sb = sb("bv_sb", [P, D])
        bo_sb = sb("bo_sb", [P, D])
        xbo_sb = sb("xbo_sb", [P, D])
        ident = sb("ident", [P, P])
        identb = sb("identb", [P, P], BF16)
        half = sb("half", [P, 1])
        parts_ctx = [parts_a[:, :, :],
                     probs_flat[:, 3328:4096].bitcast(BF16).rearrange("p (q t) -> p q t", q=3)]
        parts_q = [parts_a[:, :, :],
                   wself_sb[:, :, :].rearrange("p k n -> p (k n)")[:, 0:768].bitcast(BF16)
                   .rearrange("p (q t) -> p q t", q=3)]
        logits = sb("logits", [P, TB, E])
        wself_flat = wself_sb[:, :, :].rearrange("p k n -> p (k n)")
        sink = wself_flat[:, 768:1024].rearrange("p (b e) -> p b e", b=TB)
        turned = wself_flat[0:E, 1024:1280].rearrange("p (a n) -> p a n", a=2)
        ones = late_region[:, 0:P]
        tmp16 = late_region[:, P:P + 4 * E].rearrange("p (a e) -> p a e", a=4)
        temp = sb("temp", [P, 2])
        affin = logits
        affin_r = sink.rearrange("p b e -> p (b e)")
        chunk_v = o_region[:, 0:CHUNK]
        best_v = o_region[:, CHUNK:CHUNK + CAP]
        best_i = o_region[:, CHUNK + CAP:CHUNK + 2 * CAP].bitcast(U32)
        best_f = o_region[:, CHUNK + 2 * CAP:CHUNK + 3 * CAP]
        cand_v = o_region[0:E, 512:512 + NCH * CAP]
        cand_i = o_region[0:E, 1024:1024 + NCH * CAP]
        tops = shift_t[0:E, :].bitcast(F32)[:, 0:3 * CAP].rearrange("p (a n) -> p a n", a=3)
        chunk_steps = late_region[:, P + 4 * E:P + 4 * E + NCH]
        chunk_base = late_region[:, P + 4 * E + NCH:P + 4 * E + NCH + 1]
        picked_affin = late_region[:, 256:256 + E // 2 * E].rearrange("p (i e) -> p i e", e=E)
        idx_gather = sb("idx_gather", [P, E // 2], U32)
        idx_scatter = sb("idx_scatter", [CAP, E], U32)
        h_sb = [even_region[:, 0:1024], self_region[:, 0:1024]]
        h_t = [even_region[:, 1024:2048], self_region[:, 1024:2048]]
        b1_sb = [even_region[:, 2048:3072], even_region[:, 3072:4096],
                 xn_t[:, :, :].rearrange("p k n -> p (k n)")[:, 0:FF]]
        x_e = [self_region[:, 2048 + D * r:2048 + D * (r + 1)] for r in range(2)]
        x_e += [w[:, k, :] for w in (wo_sb, wxq_sb, wxo_sb) for k in range(DK)]
        x_et = [self_region[:, 2560 + 256 * r:2816 + 256 * r].rearrange("p (k n) -> p k n", k=DK) for r in range(2)]
        y_e = x_e
        b2_sb = [o_region[:, 256 * r:256 * r + 256] for r in range(NBIAS)]

        ps = [ctx.enter_context(nc.psum_tensor(f"scores{r}", [P, 2, TILE], F32)) for r in range(2)]
        po = ctx.enter_context(nc.psum_tensor("po", [P, TILE], F32))
        pg = [ctx.enter_context(nc.psum_tensor(f"g{r}", [P, TILE], F32)) for r in range(3)]

        s_w = {n: sem(f"w_{n}") for n in ("ctx", "xk", "xv", "self", "rest")}
        const_ready = sem("const_ready")
        v_ones = sem("v_ones")
        k_ones = sem("k_ones")
        g_full = sem("g_full")
        g_free = sem("g_free")
        dve_step = sem("dve_step")
        scores_full = sem("scores_full")
        exp_done = sem("exp_done")
        mask_done = sem("mask_done")
        pv_done = sem("pv_done")
        o_free = sem("o_free")
        x_loaded = [sem(f"x_loaded{r}") for r in range(4)]
        x_biased = sem("x_biased")
        x_stored = [sem(f"x_stored{r}") for r in range(4)]
        var_ready = sem("var_ready")
        rstd_ready = sem("rstd_ready")
        xn_ready = sem("xn_ready")
        xn_stored = [sem(f"xn_stored{r}") for r in range(2)]
        lines_split = sem("lines_split")
        line_stored = sem("line_stored")
        lines_loaded = [sem(f"lines_loaded{j}") for j in range(NT)]
        parts_ready = sem("parts_ready")
        parts_stored = [sem(f"parts_stored{r}") for r in range(2)]
        ctx_loaded = sem("ctx_loaded")
        query_loaded = [sem(f"query_loaded{j}") for j in range(NT)]
        shift_split = sem("shift_split")
        shift_stored = sem("shift_stored")
        shift_loaded = [sem(f"shift_loaded{j}") for j in range(NT)]
        temp_ready = sem("temp_ready")
        sink_ready = sem("sink_ready")
        sink_act = sem("sink_act")
        router_pe = sem("router_pe")
        picked = sem("picked")
        affin_stored = sem("affin_stored")
        gates_gathered = [sem(f"gates_gathered{i}") for i in range(E // 2)]
        gathered = [sem(f"gathered{i}") for i in range(E // 2)]
        bias_loaded = [sem(f"bias_loaded{r}") for r in range(NBIAS)]
        h_turned = sem("h_turned")
        gelu_done = sem("gelu_done")
        y_ready = sem("y_ready")
        scattered = sem("scattered")
        w1_loaded = [sem(f"w1_loaded{s}") for s in range(NSLOT)]
        w2_loaded = [sem(f"w2_loaded{s}") for s in range(NSLOT)]

        def g_at(step):
            return G_USE[step]

        loads = {}
        for st in PLAN:
            if st[0] == "x_load":
                loads[st[3]] = st

        def count_before(test, step):
            return sum(1 for s in PLAN[:where[step]] if test(s))

        splits = [s for s in PLAN if s[0] in ("ctx_k", "x_query")]
        norms = [s for s in PLAN if s[0] == "norm"]
        stats = [(s[1], s[2], s[3]) for s in PLAN if s[0] == "stats" or (s[0] == "out_proj" and s[1] == "cross")]
        joins = [s for s in PLAN if s[0] == "out_proj"]
        biased = [s for s in PLAN if s[0] == "x_load" and s[1] in ("self", "cross")]
        masks = [n for n, (kind, j, g, i, _) in enumerate(QUADS) if kind == "self" and i >= BPT * j]
        norm_no = {s[3]: n for n, s in enumerate(norms)}
        stat_no = {s[2]: n for n, s in enumerate(stats)}
        join_no = {s[3]: n for n, s in enumerate(joins)}
        bias_no = {s[3]: n for n, s in enumerate(biased)}
        mask_no = {n: m for m, n in enumerate(masks)}
        last_quad = {}
        for n, (kind, j, g, i, end) in enumerate(QUADS):
            last_quad[kind, j] = n
        evacs = [s for s in PLAN if s[0] == "o_evac"]
        x_stores = [sum(1 for s in joins if s[3] % 4 == r) for r in range(4)]
        evac_no = {(s[1], s[2], s[3]): n for n, s in enumerate(evacs)}

        def quad_cols(n):
            kind, j, g, i, _ = QUADS[n]
            off = max(0, i - BPT * j) * P if kind == "self" else 0
            rows = min(P, S - i * P) if kind == "cross" else P
            return off, rows

        ctx_splits = sum(1 for s in splits if s[0] == "ctx_k")
        ctx_parts = [-(-ctx_splits // 2), ctx_splits // 2]
        ctx_users = [g_at(s) for s in PLAN if s[0] in ("ctx_k", "ctx_v")]

        NG = len(G_USE)
        tail = ["col_turn", "col_back"] + [("col_sum", it) for it in range(SINK_ITERS)]
        tail += ["aff", "cand_v", "cand_i", "tops", ("xe", 0), ("h", 0, 0), ("h", 0, 1)]
        for i in range(E // 2):
            if i + 1 < E // 2:
                tail += [("xe", i + 1), ("h", i + 1, 0), ("h", i + 1, 1)]
            tail += [("y", i)]
        TG = {s: NG + n for n, s in enumerate(tail)}

        def tail_full(dve, name):
            dve.wait_ge(g_full, TG[name] + 1)
            return pg[TG[name] % 3]

        def tail_bank(pe, name):
            pe.wait_ge(g_free, TG[name] - 2)
            return pg[TG[name] % 3]

        def load_w1(eng, e):
            s = e % NSLOT
            eng.dma_start(slots[s][:, 0:2048].rearrange("p (k n) -> p k n", k=2),
                          w1[e].rearrange("(k p) n -> p k n", p=P)).then_inc(w1_loaded[s], 16)

        def load_w2(eng, e):
            s = e % NSLOT
            eng.dma_start(slots[s][:, 2048:4096].rearrange("p (k n) -> p k n", k=8),
                          w2[e].rearrange("(k p) n -> p k n", p=P)).then_inc(w2_loaded[s], 16)

        def load_line_side(eng, j, side):
            cols = slice(j * TILE, (j + 1) * TILE)
            slots_of, dst = ((Q_SLOTS, q_line[j % 2]), (K_SLOTS, k_line[:, :, cols]))[side]
            for s, part in enumerate(slots_of):
                src = line_d[side, part, :, cols].rearrange("(a e c) t -> c e a t", e=2, c=NC)
                for e in range(2):
                    eng.dma_start(dst[64 * e + s * NC:64 * e + (s + 1) * NC, :, :],
                                  src[:, e, :, :]).then_inc(lines_loaded[j], 16)

        block = ctx.enter_context(nc.Block())

        @block.sync
        def _(sp):
            sp.dma_start(wself_sb[:, :, :], w_self.rearrange("(k p) n -> p k n", p=P)).then_inc(s_w["self"], 16)
            stored = {}
            store_count = [0] * 4
            line_stores = 0
            n_parts = [0, 0]
            shift_stores = 0
            xn_store_count = [0, 0]

            def plain_load(step):
                _, kind, b, u = step
                r = u % 4
                if u >= 4:
                    prev = loads[u - 4]
                    if prev[1] != "self":
                        sp.wait_ge(xn_ready, norm_no[u - 4] + 1)
                    if prev[1] in ("self", "cross"):
                        sp.wait_ge(x_stored[r], 16 * store_count[r])
                src = x if kind in ("prep", "self") else x1_d
                if kind in ("query", "cross"):
                    us, cnt = stored[b]
                    sp.wait_ge(x_stored[us % 4], 16 * cnt)
                sp.dma_start(xb[:, r, :], src[b * P:(b + 1) * P, :]).then_inc(x_loaded[r], 16)

            for step in PLAN:
                kind = step[0]
                if kind == "x_load":
                    plain_load(step)
                elif kind == "stats" and step[3] == 0:
                    sp.dma_start(ctx_sb, ctx_t.rearrange("(k p) s -> p k s", p=P)).then_inc(s_w["ctx"], 16)
                    sp.dma_start(wxk_sb, w_xk.rearrange("(k p) n -> p k n", p=P)).then_inc(s_w["xk"], 16)
                    sp.dma_start(wxv_sb, w_xv.rearrange("(k p) n -> p k n", p=P)).then_inc(s_w["xv"], 16)
                    for dst, src in ((wo_sb, w_o), (wxq_sb, w_xq), (wxo_sb, w_xo)):
                        sp.dma_start(dst[:, :, :], src.rearrange("(k p) n -> p k n", p=P)).then_inc(s_w["rest"], 16)
                    sp.dma_start(gate_sb[:, :, :], gate_t.rearrange("(k p) n -> p k n", p=P)).then_inc(s_w["rest"], 16)
                    for dst, src in ((bv_sb, bv), (bo_sb, bo), (xbo_sb, xbo)):
                        sp.dma_start(dst[:, :], src.partition_broadcast(P)).then_inc(s_w["rest"], 16)
                    sp.dma_start(temp[:, 0:1], log_temp.partition_broadcast(P)).then_inc(s_w["rest"], 16)
                elif kind in ("ctx_k", "x_query"):
                    n = splits.index(step)
                    r = n % 2
                    sp.wait_ge(parts_ready, n + 1)
                    if kind == "ctx_k":
                        _, t, m = step
                        n_keys = min(TILE, S - t * TILE)
                        dst = xk_d[:, m * P:(m + 1) * P, t * TILE:t * TILE + n_keys]
                        src = parts_ctx[r][:, :, 0:n_keys]
                    else:
                        _, j, m = step
                        dst = xq_d[:, m * P:(m + 1) * P, j * TILE:(j + 1) * TILE]
                        src = parts_q[r]
                    sp.dma_start(dst.rearrange("q p n -> p q n"), src).then_inc(parts_stored[r], 16)
                    n_parts[r] += 1
                elif kind == "ctx_load":
                    t = step[1]
                    n_keys = min(TILE, S - t * TILE)
                    for r in range(2):
                        sp.wait_ge(parts_stored[r], 16 * n_parts[r])
                    for s, part in enumerate(K_SLOTS):
                        sp.dma_start(k_cross[s * DH:(s + 1) * DH, :, t * TILE:t * TILE + n_keys],
                                     xk_d[part, :, t * TILE:t * TILE + n_keys].rearrange("(h d) n -> d h n", d=DH)
                                     ).then_inc(ctx_loaded, 16)
                elif kind == "query_load":
                    j = step[1]
                    for r in range(2):
                        sp.wait_ge(parts_stored[r], 16 * n_parts[r])
                    if j == 1:
                        sp.wait_ge(pv_done, last_quad["self", NT - 1] + 1)
                    if j >= 2:
                        sp.wait_ge(pv_done, last_quad["cross", j - 2] + 1)
                    for s, part in enumerate(Q_SLOTS):
                        sp.dma_start(q_cross[j % 2][s * DH:(s + 1) * DH, :, :],
                                     xq_d[part, :, j * TILE:(j + 1) * TILE].rearrange("(h d) n -> d h n", d=DH)
                                     ).then_inc(query_loaded[j], 16)
                elif kind == "line_turn":
                    b = step[1]
                    sp.wait_ge(g_free, g_at(step) + 1)
                    sp.dma_start(line_d[:, :, :, b * P:(b + 1) * P].rearrange("a q n t -> n (a q) t"),
                                 line_t[:, :, :]).then_inc(line_stored, 16)
                    line_stores += 1
                elif kind == "line_load":
                    j = step[1]
                    sp.wait_ge(line_stored, 16 * line_stores)
                    if j >= 2:
                        sp.wait_ge(pv_done, last_quad["self", j - 2] + 1)
                    load_line_side(sp, j, 0)
                    if j:
                        load_line_side(sp, j, 1)
                elif kind == "out_proj":
                    _, which, b, u = step
                    r = u % 4
                    sp.wait_ge(g_free, g_at(step) + 1)
                    sp.dma_start((x1_d if which == "self" else out)[b * P:(b + 1) * P, :],
                                 xb[:, r, :]).then_inc(x_stored[r], 16)
                    store_count[r] += 1
                    if which == "self":
                        stored[b] = (u, store_count[r])
                elif kind == "norm" and step[1] == "cross":
                    _, _, b, u = step
                    r = norm_no[u] % 2
                    sp.wait_ge(xn_ready, norm_no[u] + 1)
                    sp.dma_start(xn_d[b * P:(b + 1) * P, :], xn[:, r, :]).then_inc(xn_stored[r], 16)
                    xn_store_count[r] += 1
                elif kind == "shift_load":
                    j = step[1]
                    sp.wait_ge(g_free, g_at(("shift_turn", j, BPT * j + BPT - 1)) + 1)
                    cols = slice(j * TILE, (j + 1) * TILE)
                    sp.dma_start(shift_d[:, :, cols].rearrange("q h t -> (q h) t"),
                                 shift_t[:, :]).then_inc(shift_stored, 16)
                    shift_stores += 1
                    sp.wait_ge(shift_stored, 16 * shift_stores)
                    sp.dma_start(q_cross[j % 2][NS * DH:NS * DH + 3, :, :],
                                 shift_d[:, :, cols]).then_inc(shift_loaded[j], 16)
            for r in range(4):
                sp.wait_ge(x_stored[r], 16 * store_count[r])
            for r in range(2):
                sp.wait_ge(xn_stored[r], 16 * xn_store_count[r])
            sp.wait_ge(pv_done, len(QUADS))
            for e in range(3, NSLOT):
                load_w1(sp, e)
                load_w2(sp, e)

            def load_biases(i):
                for e in range(2):
                    rows = slice(CAP * e, CAP * (e + 1))
                    for dst, src in ((b1_sb, b1), (b2_sb, b2)):
                        sp.dma_start(dst[i % NBIAS][rows, :], src[2 * i + e].partition_broadcast(CAP)
                                     ).then_inc(bias_loaded[i % NBIAS], 16)

            sp.wait_ge(router_pe, 3 + SINK_ITERS)
            sp.dma_start(affin_d.rearrange("(b p) e -> p b e", p=P), affin[:, :, :]).then_inc(affin_stored, 16)

            sp.wait_ge(g_free, TG["tops"] + 1)
            for i in range(NBIAS):
                load_biases(i)

            def next_w1(i):
                sp.wait_ge(g_full, TG["h", i, 1] + 1)
                for e in range(2 * i + NSLOT, 2 * i + 2 + NSLOT):
                    load_w1(sp, e)

            later = (E - NSLOT) // 2
            next_w1(0)
            for i in range(E // 2 - NBIAS):
                if i + 1 < later:
                    next_w1(i + 1)
                sp.wait_ge(g_free, TG["y", i] + 1)
                load_biases(i + NBIAS)
                if i < later:
                    for e in range(2 * i + NSLOT, 2 * i + 2 + NSLOT):
                        load_w2(sp, e)

        @block.gpsimd
        def _(pool):
            pool.memset(half[:, :], -0.5).then_inc(const_ready, 1)
            pool.memset(ident[:, :], 0.0).then_inc(const_ready, 1)
            pool.memset(identb[:, :], 0.0).then_inc(const_ready, 1)
            pool.wait_ge(const_ready, 3)
            for m in (ident, identb):
                pool.affine_select(out=m[:, :], in_=m[:, :], compare_op=ALU.not_equal, fill=1.0, base=0,
                                   pattern=[[-1, P]], channel_multiplier=1).then_inc(const_ready, 1)
            pool.wait_ge(const_ready, 5)
            pool.memset(cross_region[NS * DH:P, 0:H * SP // 2], BF16_ONES).then_inc(k_ones, 1)
            pool.wait_ge(k_ones, 1)
            for step in PLAN:
                kind = step[0]
                if kind == "stats" or (kind == "out_proj" and step[1] == "cross"):
                    u = step[3]
                    pool.wait_ge(var_ready, stat_no[u] + 1)
                    pool.tensor_tensor(rstd[:, u % 4:u % 4 + 1], mv[:, u % 4, 1:2], half[:, 0:1],
                                       ALU.pow).then_inc(rstd_ready, 1)
                elif kind == "x_load" and step[1] in ("self", "cross"):
                    u = step[3]
                    if u == biased[0][3]:
                        pool.wait_ge(s_w["rest"], 128)
                    pool.wait_ge(x_loaded[u % 4], 16 * (u // 4 + 1))
                    pool.tensor_tensor(xb[:, u % 4, :], xb[:, u % 4, :], (bo_sb if step[1] == "self" else xbo_sb)[:, :],
                                       ALU.add).then_inc(x_biased, 1)
                elif kind == "scores" and step[1] in mask_no:
                    _, n, e = step
                    off, _ = quad_cols(n)
                    s = 2 * n + e
                    pool.wait_ge(exp_done, s + 1)
                    d = probs[:, s % 4, :, off:off + P]
                    pool.affine_select(out=d, in_=d, compare_op=ALU.is_ge, fill=0.0, base=0,
                                       pattern=[[0, 2], [1, P]], channel_multiplier=-1).then_inc(mask_done, 1)
            pool.wait_ge(line_stored, 16 * TB)
            pool.memset(ones[:, :], 1.0).then_inc(const_ready, 1)
            pool.memset(chunk_steps[:, 0:NCH - 1], float(CHUNK)).then_inc(const_ready, 1)
            pool.memset(chunk_steps[:, NCH - 1:NCH], 1.0).then_inc(const_ready, 1)
            pool.wait_ge(const_ready, 8)
            pool.affine_select(out=chunk_steps[:, 0:NCH - 1], in_=chunk_steps[:, 0:NCH - 1], compare_op=ALU.is_ge,
                               fill=0.0, base=-E, pattern=[[-E, NCH - 1]], channel_multiplier=1
                               ).then_inc(const_ready, 1)

            pool.wait_ge(g_free, TG["tops"] + 1)
            pool.wait_ge(picked, 2)
            pool.wait_ge(affin_stored, 16)
            for r in range(2):
                pool.wait_ge(xn_stored[r], 16 * TB // 2)
            for r in range(4):
                pool.wait_ge(x_stored[r], 16 * x_stores[r])
            for i in range(E // 2):
                pool.indirect_dma_start(
                    x_e[i], None, xn_d, bass.IndirectOffsetOnAxis(idx_gather[:, i:i + 1], 0)).then_inc(gathered[i], 16)
                pool.indirect_dma_start(
                    picked_affin[:, i, :], None, affin_d, bass.IndirectOffsetOnAxis(idx_gather[:, i:i + 1], 0)
                ).then_inc(gates_gathered[i], 16)
            for i in range(E // 2):
                for e in range(2):
                    pool.wait_ge(y_ready, 2 * i + e + 1)
                    if 2 * i + e:
                        pool.wait_ge(scattered, 16 * (2 * i + e))
                    rows = slice(CAP * e, CAP * (e + 1))
                    pool.indirect_dma_start(
                        out, bass.IndirectOffsetOnAxis(idx_scatter[:, 2 * i + e:2 * i + e + 1], 0), y_e[i][rows, :], None,
                        compute_op=ALU.add).then_inc(scattered, 16)
            pool.wait_ge(scattered, 16 * E)

        @block.scalar
        def _(act):
            act.wait_ge(s_w["rest"], 128)
            act.activation(temp[:, 1:2], temp[:, 0:1], ACT.Exp).then_inc(temp_ready, 1)
            for step in PLAN:
                if step[0] == "scores":
                    _, n, e = step
                    off, rows = quad_cols(n)
                    s = 2 * n + e
                    if s == 0:
                        act.wait_ge(g_free, max(ctx_users) + 1)
                        for r in range(2):
                            act.wait_ge(parts_stored[r], 16 * ctx_parts[r])
                    act.wait_ge(scores_full, s + 1)
                    if s >= 4:
                        act.wait_ge(pv_done, (s - 4) // 2 + 1)
                    act.activation(probs[0:rows, s % 4, :, off:], ps[s % 2][0:rows, :, off:], ACT.Exp,
                                   scale=LSCALE if QUADS[n][0] == "self" else 1.0).then_inc(exp_done, 1)
                elif step[0] == "o_evac":
                    _, which, j, gi, n = step
                    act.wait_ge(pv_done, n + 1)
                    e = evac_no[which, j, gi]
                    if e >= 4:
                        users = [g_at(s) for s in PLAN if s[0] == "o_turn" and s[1] == evacs[e - 4][1]
                                 and s[2] // BPT == evacs[e - 4][2]]
                    else:
                        users = ctx_users
                    act.wait_ge(g_full, max(users) + 1)
                    act.copy(o_sb[:, gi, :], po[:, :]).then_inc(o_free, 1)
                elif step == ("line_load", 0):
                    act.wait_ge(line_stored, 16 * BPT)
                    load_line_side(act, 0, 1)
                elif step[0] == "weights":
                    if step[1] == 0:
                        act.wait_ge(pv_done, last_quad["self", NT - 1] + 1)
                    load_w1(act, step[1])
                    load_w2(act, step[1])
            act.wait_ge(sink_ready, 1)
            act.activation(affin[:, :, :], sink[:, :, :], ACT.Exp).then_inc(sink_act, 1)
            act.wait_ge(sink_ready, 2)
            act.activation(tmp16[:, 3, :], tmp16[:, 2, :], ACT.Ln).then_inc(sink_act, 1)
            act.wait_ge(g_free, TG["col_back"] + 1)
            act.activation(affin[:, :, :], sink[:, :, :], ACT.Exp).then_inc(sink_act, 1)
            for i in range(E // 2):
                act.wait_ge(h_turned, i + 1)
                if i >= 2:
                    act.wait_ge(g_full, TG["y", i - 2] + 1)
                act.activation(h_t[i % 2], ps[i % 2][:, :, :].rearrange("p a b -> p (a b)"),
                               ACT.Gelu_apprx_tanh).then_inc(gelu_done, 1)


        @block.vector
        def _(dve):
            steps = [0]

            def link(ins):
                steps[0] += 1
                ins.then_inc(dve_step, 1)
                dve.wait_ge(dve_step, steps[0])

            def full(step):
                dve.wait_ge(g_full, g_at(step) + 1)
                return pg[g_at(step) % 3]

            def rsqrt(y, v, t):
                yi, vi = y.bitcast(I32), v.bitcast(I32)
                link(dve.tensor_scalar(yi, vi, 1, None, ALU.logical_shift_right))
                link(dve.tensor_scalar(yi, yi, -1.0, float(0x5F3759DF), ALU.mult, ALU.add))
                for _ in range(3):
                    link(dve.tensor_tensor(t, y, y, ALU.mult))
                    link(dve.tensor_tensor(t, t, v, ALU.mult))
                    link(dve.tensor_scalar(t, t, -0.5, 1.5, ALU.mult, ALU.add))
                    link(dve.tensor_tensor(y, y, t, ALU.mult))

            def block_stats(u):
                r = u % 4
                if u >= 4 and loads[u - 4][1] != "self":
                    dve.wait_ge(xn_ready, norm_no[u - 4] + 1)
                link(dve.bn_stats(bn[:, r, :], xb[:, r, :]))
                link(dve.bn_aggr(mv[:, r, :], bn[:, r, :]))
                dve.tensor_scalar(mv[:, r, 1:2], mv[:, r, 1:2], EPS, None, ALU.add).then_inc(var_ready, 1)

            def split(src, parts, n, g_count):
                link(dve.tensor_copy(parts[:, 0, 0:n], src))
                dve.tensor_tensor(rest[:, 0:n], src, parts[:, 0, 0:n], ALU.subtract).then_inc(g_free, 1)
                dve.wait_ge(g_free, g_count)
                link(dve.tensor_copy(parts[:, 1, 0:n], rest[:, 0:n]))
                dve.tensor_tensor(parts[:, 2, 0:n], rest[:, 0:n], parts[:, 1, 0:n],
                                  ALU.subtract).then_inc(parts_ready, 1)

            def parts_free(step):
                n = splits.index(step)
                if n >= 2:
                    dve.wait_ge(parts_stored[n % 2], 16 * (n // 2))
                    dve.wait_ge(parts_ready, n)
                return n % 2

            for v in (v_self, v_cross):
                dve.memset(v[:, :, H * VW:], 0.0).then_inc(v_ones, 1)
            for v in (v_self, v_cross):
                dve.memset(v[:, :, 0:H * VW].rearrange("p b (h v) -> p b h v", h=H)[:, :, :, DH],
                           1.0).then_inc(v_ones, 1)
            for step in PLAN:
                kind = step[0]
                if kind == "stats":
                    u = step[3]
                    dve.wait_ge(x_loaded[u % 4], 16 * (u // 4 + 1))
                    block_stats(u)
                elif kind == "norm":
                    u = step[3]
                    n = norm_no[u]
                    r = n % 2
                    dve.wait_ge(rstd_ready, stat_no[u] + 1)
                    if n >= 2:
                        dve.wait_ge(g_full, g_at(("x_turn", *norms[n - 2][1:])) + 1)
                        dve.wait_ge(xn_ready, n - 1)
                        stores = sum(1 for s in norms[r:n - 1:2] if s[1] == "cross")
                        if stores:
                            dve.wait_ge(xn_stored[r], 16 * stores)
                    dve.tensor_scalar(xn[:, r, :], xb[:, u % 4, :], mv[:, u % 4, 0:1], rstd[:, u % 4:u % 4 + 1],
                                      ALU.subtract, ALU.mult).then_inc(xn_ready, 1)
                elif kind == "carry":
                    if step[1] == 0:
                        link(dve.memset(xn_t[:, :, 0:1], 0.0))
                    else:
                        link(dve.tensor_copy(xn_t[:, :, 0], carry[:, :]))
                elif kind == "x_turn":
                    g = full(step)
                    c = 1 + (step[2] % BPT) * P
                    dve.tensor_copy(xn_t[:, :, c:c + P], g[:, 0:DK * P].rearrange("p (k n) -> p k n", k=DK)
                                    ).then_inc(g_free, 1)
                elif kind == "carry_out":
                    dve.wait_ge(g_free, g_at(("project", BPT * step[1] + BPT - 1)))
                    link(dve.tensor_copy(carry[:, :], xn_t[:, :, TILE]))
                elif kind == "project":
                    b = step[1]
                    if b == 0:
                        dve.wait_ge(s_w["rest"], 128)
                        dve.wait_ge(v_ones, 4)
                    g = full(step)
                    link(dve.tensor_tensor(v_self[:, b, 0:H * VW].rearrange("p (h v) -> p h v", h=H)[:, :, 0:DH],
                                           g[:, 256:512].rearrange("p (h d) -> p h d", h=H),
                                           bv_sb[:, :].rearrange("p (h d) -> p h d", h=H), ALU.add))
                    dve.tensor_copy(raw[:, b % BPT, :], g[:, 0:256]).then_inc(g_free, 1)
                elif kind == "lines":
                    j = step[1]
                    dve.wait_ge(g_free, g_at(("project", BPT * j + BPT - 1)) + 1)
                    if j:
                        dve.wait_ge(lines_split, j)
                    comp = raw.rearrange("p b (s q h i) -> p b s q h i", s=2, q=2, i=4)
                    lv = lines.rearrange("p (b s) h c -> p b s h c", s=2)
                    tv = lines_t.rearrange("p (b s) h c -> p b s h c", s=2)
                    for side, pairs in ((0, Q_PAIRS), (1, K_PAIRS)):
                        for c, (a, z) in enumerate(pairs):
                            dve.tensor_tensor(lv[:, :, side, :, c], comp[:, :, side, 0, :, a],
                                              comp[:, :, side, 1, :, z], ALU.mult)
                            last = dve.tensor_tensor(tv[:, :, side, :, c], comp[:, :, side, 0, :, z],
                                                     comp[:, :, side, 1, :, a], ALU.mult)
                    link(last)
                    flat = lines.rearrange("p s h c -> p (s h c)")
                    flat_t = lines_t.rearrange("p s h c -> p (s h c)")
                    link(dve.tensor_tensor(flat, flat, flat_t, ALU.subtract))
                    link(dve.tensor_tensor(flat_t, flat, flat, ALU.mult))
                    link(dve.reduce_sum(line_n2, lines_t.rearrange("p s h c -> p (s h) c"), AX_X))
                    link(dve.tensor_scalar(line_n2, line_n2, 1e-24, None, ALU.max))
                    rsqrt(line_rn, line_n2, flat_t[:, 0:P])
                    if j:
                        dve.wait_ge(g_full, g_at(("line_turn", BPT * j - 1)) + 1)
                    l3 = lines.rearrange("p s h c -> p (s h) c")
                    link(dve.tensor_tensor(l3, l3, line_rn.unsqueeze(2).broadcast_to((P, 8 * H, NC)), ALU.mult))
                    l2 = lines.rearrange("p s h c -> p s (h c)")
                    t2 = lines_t.rearrange("p s h c -> p s (h c)")
                    link(dve.tensor_copy(line_parts[:, :, 0, :], l2))
                    link(dve.tensor_tensor(t2, l2, line_parts[:, :, 0, :], ALU.subtract))
                    link(dve.tensor_copy(line_parts[:, :, 1, :], t2))
                    dve.tensor_tensor(line_parts[:, :, 2, :], t2, line_parts[:, :, 1, :],
                                      ALU.subtract).then_inc(lines_split, 1)
                elif kind == "line_turn":
                    b = step[1]
                    g = full(step)
                    if b:
                        dve.wait_ge(line_stored, 16 * b)
                    dve.tensor_copy(line_t[:, :, :], g[0:H * NC, 0:384].bitcast(BF16)
                                    .rearrange("p (a t) -> p a t", a=6)).then_inc(g_free, 1)
                elif kind == "ctx_k":
                    _, t, m = step
                    g = full(step)
                    r = parts_free(step)
                    n_keys = min(TILE, S - t * TILE)
                    split(g[:, 0:n_keys], parts_ctx[r], n_keys, g_at(step) + 1)
                elif kind == "ctx_v":
                    b = step[1]
                    if b == 0:
                        dve.wait_ge(v_ones, 4)
                    g = full(step)
                    nb = min(2, SB - b)
                    rows = min(P, S - b * P)
                    dve.tensor_copy(
                        v_cross[0:rows, b:b + nb, 0:H * VW].rearrange("p b (h v) -> p b h v", h=H)[:, :, :, 0:DH],
                        g[0:rows, 0:nb * D].rearrange("p (b h d) -> p b h d", b=nb, h=H)).then_inc(g_free, 1)
                elif kind == "o_turn":
                    g = full(step)
                    gv = g[:, :].rearrange("p (h r) -> p h r", r=32)
                    link(dve.reciprocal(rsum[:, :], gv[:, :, DH]))
                    dve.tensor_tensor(attn[:, :].rearrange("p (h d) -> p h d", h=H), gv[:, :, 0:DH],
                                      rsum[:, :].unsqueeze(2).broadcast_to((P, H, DH)), ALU.mult).then_inc(g_free, 1)
                elif kind == "a_turn":
                    g = full(step)
                    dve.tensor_copy(attn_t[:, :, :], g[:, 0:DK * P].rearrange("p (k n) -> p k n", k=DK)
                                    ).then_inc(g_free, 1)
                elif kind == "out_proj":
                    _, which, b, u = step
                    g = full(step)
                    dve.wait_ge(x_biased, bias_no[u] + 1)
                    dve.tensor_tensor(xb[:, u % 4, :], g[:, 0:D], xb[:, u % 4, :], ALU.add).then_inc(g_free, 1)
                    if which == "cross":
                        dve.wait_ge(g_free, g_at(step) + 1)
                        block_stats(u)
                elif kind == "x_query":
                    g = full(step)
                    r = parts_free(step)
                    if step[1] == 0:
                        dve.wait_ge(g_full, g_at(("project", TB - 1)) + 1)
                    split(g[:, :], parts_q[r], TILE, g_at(step) + 1)
                elif kind == "max":
                    _, j, b, h, c = step
                    g = full(step)
                    n_keys = min(TILE, S - c * TILE)
                    dve.reduce_max(mx[:, b % 2, h, c:c + 1], g[:, 0:n_keys], AX_X).then_inc(g_free, 1)
                elif kind == "shift":
                    _, j, b = step
                    if b:
                        dve.wait_ge(g_full, g_at(("shift_turn", (b - 1) // BPT, b - 1)) + 1)
                    dve.wait_ge(g_free, g_at(("max", j, b, H - 1, ST - 1)) + 1)
                    f0, f1 = shift_f[:, 0, :], shift_f[:, 1, :]
                    link(dve.reduce_max(f0, mx[:, b % 2, :, :], AX_X))
                    link(dve.tensor_scalar(f1, f0, -1.0, None, ALU.mult))
                    link(dve.tensor_copy(shift_parts[:, 0, :], f1))
                    link(dve.tensor_tensor(f0, f1, shift_parts[:, 0, :], ALU.subtract))
                    link(dve.tensor_copy(shift_parts[:, 1, :], f0))
                    dve.tensor_tensor(shift_parts[:, 2, :], f0, shift_parts[:, 1, :],
                                      ALU.subtract).then_inc(shift_split, 1)
                elif kind == "shift_turn":
                    _, j, b = step
                    g = full(step)
                    if b % BPT == 0 and j:
                        dve.wait_ge(shift_stored, 16 * j)
                    dve.tensor_copy(shift_t[:, (b % BPT) * P:(b % BPT + 1) * P],
                                    g[0:3 * H, 0:P // 2].bitcast(BF16)).then_inc(g_free, 1)
                elif kind == "gate":
                    b = step[1]
                    g = full(step)
                    dve.tensor_copy(logits[:, b, :], g[:, 0:E]).then_inc(g_free, 1)

            def col_view(ap):
                return ap.rearrange("p b e -> p e b")

            def over_experts(v):
                return v.unsqueeze(2).broadcast_to((P, TB, E))

            def over_blocks(v):
                return v.unsqueeze(1).broadcast_to((P, TB, E))

            row, col = tmp16[:, 0, :], tmp16[:, 1, :]
            dve.wait_ge(const_ready, 6)
            dve.wait_ge(temp_ready, 1)
            link(dve.reciprocal(temp[:, 0:1], temp[:, 1:2]))
            dve.wait_ge(g_free, NG)
            link(dve.tensor_scalar(sink[:, :, :], logits[:, :, :], temp[:, 0:1], None, ALU.mult))
            link(dve.reduce_max(row, sink[:, :, :], AX_X))
            dve.tensor_tensor(sink[:, :, :], sink[:, :, :], over_experts(row), ALU.subtract).then_inc(sink_ready, 1)
            dve.wait_ge(sink_act, 1)
            link(dve.reduce_sum(row, affin[:, :, :], AX_X))
            dve.tensor_copy(tmp16[:, 2, :], row).then_inc(sink_ready, 1)
            dve.wait_ge(sink_act, 2)
            link(dve.tensor_tensor(sink[:, :, :], sink[:, :, :], over_experts(tmp16[:, 3, :]), ALU.subtract))
            dve.reduce_max(col, col_view(sink[:, :, :]), AX_X).then_inc(router_pe, 1)
            g = tail_full(dve, "col_turn")
            dve.reduce_max(turned[:, 1, 0:1], g[0:E, 0:P], AX_X).then_inc(g_free, 1)
            dve.wait_ge(g_free, TG["col_turn"] + 1)
            dve.tensor_scalar(turned[:, 0, :], ones[0:E, :], turned[:, 1, 0:1], None, ALU.mult).then_inc(router_pe, 1)
            g = tail_full(dve, "col_back")
            dve.tensor_tensor(sink[:, :, :], sink[:, :, :], over_blocks(g[:, 0:E]), ALU.subtract).then_inc(g_free, 1)
            dve.wait_ge(sink_act, 3)
            for it in range(SINK_ITERS):
                if it:
                    link(dve.reduce_sum(row, affin[:, :, :], AX_X))
                    link(dve.reciprocal(row, row))
                    link(dve.tensor_tensor(affin[:, :, :], affin[:, :, :], over_experts(row), ALU.mult))
                dve.reduce_sum(col, col_view(affin[:, :, :]), AX_X).then_inc(router_pe, 1)
                g = tail_full(dve, ("col_sum", it))
                dve.reciprocal(col, g[:, 0:E]).then_inc(g_free, 1)
                dve.wait_ge(g_free, TG["col_sum", it] + 1)
                last = dve.tensor_tensor(affin[:, :, :], affin[:, :, :], over_blocks(col), ALU.mult)
                if it < SINK_ITERS - 1:
                    link(last)
                else:
                    last.then_inc(router_pe, 1)
            dve.wait_ge(router_pe, 3 + SINK_ITERS)
            dve.tensor_copy(affin_r.rearrange("p (f c e) -> p c f e", f=2, e=E),
                            affin.rearrange("p (c f) e -> p c f e", f=2)).then_inc(router_pe, 1)
            dve.wait_ge(const_ready, 9)
            link(dve.reduce_sum(chunk_base, chunk_steps, AX_X))
            g = tail_full(dve, "aff")
            dve.tensor_copy(chunk_v, g[:, 0:CHUNK]).then_inc(g_free, 1)
            dve.wait_ge(g_free, TG["aff"] + 1)

            for r in range(CAP // 8):
                eight = slice(8 * r, 8 * r + 8)
                link(dve.max(best_v[:, eight], chunk_v))
                link(dve.max_index(best_i[:, eight], best_v[:, eight], chunk_v))
                if r < CAP // 8 - 1:
                    link(dve.match_replace(out=chunk_v, in_to_replace=best_v[:, eight], in_values=chunk_v,
                                           imm_value=-1.0))
            dve.tensor_scalar(best_f, best_i, chunk_base, None, ALU.add).then_inc(router_pe, 1)
            for name, cand in (("cand_v", cand_v), ("cand_i", cand_i)):
                g = tail_full(dve, name)
                dve.tensor_copy(cand, g[0:E, :]).then_inc(g_free, 1)
            dve.wait_ge(g_free, TG["cand_i"] + 1)
            for r in range(CAP // 8):
                vals = tops[:, 0, 8 * r:8 * r + 8]
                link(dve.max(vals, cand_v))
                link(dve.match_replace(out=cand_v, in_to_replace=vals, in_values=cand_v, imm_value=-1.0))
            link(dve.scalar_tensor_tensor(out=cand_i, in0=cand_v, scalar=-1.0, in1=cand_i, op0=ALU.is_equal,
                                          op1=ALU.mult))
            for r in range(CAP // 8):
                vals = tops[:, 1, 8 * r:8 * r + 8]
                link(dve.max(vals, cand_i))
                if r < CAP // 8 - 1:
                    link(dve.match_replace(out=cand_i, in_to_replace=vals, in_values=cand_i, imm_value=0.0))
            dve.tensor_scalar(tops[:, 2, :], tops[:, 1, :], -1.0, None, ALU.add).then_inc(router_pe, 1)
            g = tail_full(dve, "tops")
            for e in range(2):
                dve.tensor_copy(idx_gather[CAP * e:CAP * (e + 1), :],
                                g[0:CAP, 0:E].rearrange("p (i e) -> p e i", e=2)[:, e, :]).then_inc(picked, 1)
            dve.tensor_copy(idx_scatter[:, :], g[0:CAP, 0:E]).then_inc(g_free, 1)

            def expert_in(i):
                g = tail_full(dve, ("xe", i))
                dve.tensor_copy(x_et[i % 2], g[:, 0:DK * P].rearrange("p (k n) -> p k n", k=DK)).then_inc(g_free, 1)

            def hidden(i):
                dve.wait_ge(bias_loaded[i % NBIAS], 64 * (i // NBIAS + 1))
                if i >= 2:
                    dve.wait_ge(h_turned, i - 1)
                for f in range(2):
                    g = tail_full(dve, ("h", i, f))
                    dve.tensor_tensor(h_sb[i % 2][:, f * TILE:(f + 1) * TILE], g[:, :],
                                      b1_sb[i % NBIAS][:, f * TILE:(f + 1) * TILE], ALU.add).then_inc(g_free, 1)

            def expert_out(i):
                g = tail_full(dve, ("y", i))
                if i >= 1:
                    dve.wait_ge(y_ready, 2 * i)
                dve.tensor_tensor(rest[:, 0:D], g[:, 0:D], b2_sb[i % NBIAS], ALU.add).then_inc(g_free, 1)
                dve.wait_ge(g_free, TG["y", i] + 1)
                dve.wait_ge(gates_gathered[i], 16)
                for e in range(2):
                    rows = slice(CAP * e, CAP * (e + 1))
                    dve.tensor_scalar(y_e[i][rows, :], rest[rows, 0:D], picked_affin[rows, i, 2 * i + e:2 * i + e + 1],
                                      None, ALU.mult).then_inc(y_ready, 1)

            expert_in(0)
            hidden(0)
            for i in range(E // 2):
                if i + 1 < E // 2:
                    expert_in(i + 1)
                    hidden(i + 1)
                expert_out(i)

        @block.tensor
        def _(pe):
            def bank(step):
                n = g_at(step)
                if n >= 3:
                    pe.wait_ge(g_free, n - 2)
                return pg[n % 3]

            def after(step):
                pe.wait_ge(g_free, g_at(step) + 1)

            def scores(n, e):
                kind, j, g, i, _ = QUADS[n]
                off, rows = quad_cols(n)
                if kind == "self" and g == 0 and i == 0 and e == 0:
                    pe.wait_ge(lines_loaded[j], 16 * 24)
                if kind == "cross" and g == 0 and i == 0 and e == 0:
                    pe.wait_ge(shift_loaded[j], 16)
                    pe.wait_ge(k_ones, 1)
                s = 2 * n + e
                if s >= 2:
                    pe.wait_ge(exp_done, s - 1)
                for a in range(2):
                    h = 4 * g + 2 * e + a
                    if kind == "self":
                        r = 64 * a
                        lhs = k_line[r:r + NS * NC, h // 2, i * P:(i + 1) * P]
                        rhs = q_line[j % 2][r:r + NS * NC, h // 2, off:]
                    else:
                        lhs = k_cross[0:NS * DH + 3, h, i * P:i * P + rows]
                        rhs = q_cross[j % 2][0:NS * DH + 3, h, :]
                    mm = pe.matmul(ps[s % 2][0:rows, a, off:], lhs, rhs, start=True, stop=True)
                mm.then_inc(scores_full, 1)

            def values(n):
                kind, j, g, i, end = QUADS[n]
                off, rows = quad_cols(n)
                if n in mask_no:
                    pe.wait_ge(mask_done, 2 * mask_no[n] + 2)
                else:
                    pe.wait_ge(exp_done, 2 * n + 2)
                if i == 0:
                    e = evac_no[kind, j, g]
                    if e:
                        pe.wait_ge(o_free, e)
                v = v_self if kind == "self" else v_cross
                for a in range(4):
                    h = 4 * g + a
                    s = 2 * n + a // 2
                    mm = pe.matmul(po[32 * a:32 * a + 32, off:], v[0:rows, i, h * VW:h * VW + 32],
                                   probs[0:rows, s % 4, a % 2, off:], start=(i == 0),
                                   stop=end or (kind == "self" and i >= BPT * j), skip_group_check=off > 0)
                mm.then_inc(pv_done, 1)

            pe.wait_ge(const_ready, 5)
            for step in PLAN:
                kind = step[0]
                if kind == "scores":
                    scores(step[1], step[2])
                elif kind == "pv":
                    values(step[1])
                if step not in G_USE:
                    continue
                g = bank(step)
                if kind == "ctx_k":
                    _, t, m = step
                    if step == ("ctx_k", 0, 0):
                        pe.wait_ge(s_w["ctx"], 16)
                        pe.wait_ge(s_w["xk"], 16)
                    n_keys = min(TILE, S - t * TILE)
                    for k in range(DK):
                        mm = pe.matmul(g[:, 0:n_keys], wxk_sb[:, k, m * P:(m + 1) * P],
                                       ctx_sb[:, k, t * TILE:t * TILE + n_keys], start=(k == 0), stop=(k == DK - 1))
                elif kind == "ctx_v":
                    b0 = step[1]
                    if b0 == 0:
                        pe.wait_ge(s_w["xv"], 16)
                    for b in range(b0, min(b0 + 2, SB)):
                        rows = min(P, S - b * P)
                        for k in range(DK):
                            mm = pe.matmul(g[0:rows, (b - b0) * D:(b - b0 + 1) * D], ctx_sb[:, k, b * P:b * P + rows],
                                           wxv_sb[:, k, :], start=(k == 0), stop=(k == DK - 1))
                elif kind == "x_turn":
                    u = step[3]
                    pe.wait_ge(xn_ready, norm_no[u] + 1)
                    for k in range(DK):
                        mm = pe.transpose(g[:, k * P:(k + 1) * P], xn[:, norm_no[u] % 2, k * P:(k + 1) * P], ident[:, :])
                elif kind == "project":
                    b = step[1]
                    if b == 0:
                        pe.wait_ge(s_w["self"], 16)
                        pe.wait_ge(dve_step, 1)
                    pe.wait_ge(g_free, g_at([s for s in PLAN if s[:3] == ("x_turn", "prep", b)][0]) + 1)
                    c = (b % BPT) * P
                    for k in range(DK):
                        pe.matmul(g[:, :], xn_t[:, k, c + 1:c + 1 + P], wself_sb[:, k, 0:512], start=(k == 0), stop=False)
                    for k in range(DK):
                        mm = pe.matmul(g[:, 0:P], xn_t[:, k, c:c + P], wself_sb[:, k, 512:640], start=False,
                                       stop=(k == DK - 1))
                elif kind == "line_turn":
                    b = step[1]
                    pe.wait_ge(lines_split, b // BPT + 1)
                    gb = g[:, :].bitcast(BF16)
                    for a in range(6):
                        mm = pe.transpose(gb[0:H * NC, a * P:(a + 1) * P],
                                          line_parts[:, 2 * (b % BPT) + a // 3, a % 3, :], identb[:, :])
                elif kind == "o_turn":
                    _, which, b, u = step
                    pe.wait_ge(o_free, evac_no[which, b // BPT, 3] + 1)
                    c = (b % BPT) * P
                    for gi in range(4):
                        mm = pe.transpose(g[:, gi * P:(gi + 1) * P], o_sb[:, gi, c:c + P], ident[:, :])
                elif kind == "a_turn":
                    after(("o_turn", *step[1:]))
                    for k in range(DK):
                        mm = pe.transpose(g[:, k * P:(k + 1) * P], attn[:, k * P:(k + 1) * P], ident[:, :])
                elif kind == "out_proj":
                    if step == joins[0]:
                        pe.wait_ge(s_w["rest"], 128)
                    after(("a_turn", *step[1:]))
                    for k in range(DK):
                        mm = pe.matmul(g[:, 0:D], attn_t[:, k, :], (wo_sb if step[1] == "self" else wxo_sb)[:, k, :],
                                       start=(k == 0), stop=(k == DK - 1))
                elif kind == "x_query":
                    _, j, m = step
                    after([s for s in PLAN if s[:3] == ("x_turn", "query", BPT * j + BPT - 1)][0])
                    for k in range(DK):
                        mm = pe.matmul(g[:, :], wxq_sb[:, k, m * P:(m + 1) * P], xn_t[:, k, 1:1 + TILE],
                                       start=(k == 0), stop=(k == DK - 1))
                elif kind == "max":
                    _, j, b, h, c = step
                    if b % BPT == 0 and h == 0 and c == 0:
                        pe.wait_ge(query_loaded[j], 16 * NS)
                        pe.wait_ge(ctx_loaded, 16 * NS * ST)
                    n_keys = min(TILE, S - c * TILE)
                    q = (b % BPT) * P
                    mm = pe.matmul(g[:, 0:n_keys], q_cross[j % 2][0:NS * DH, h, q:q + P],
                                   k_cross[0:NS * DH, h, c * TILE:c * TILE + n_keys], start=True, stop=True)
                elif kind == "shift_turn":
                    b = step[2]
                    pe.wait_ge(shift_split, b + 1)
                    mm = pe.transpose(g[:, :].bitcast(BF16)[0:3 * H, 0:P],
                                      shift_parts[:, :, :].rearrange("p q h -> p (q h)"), identb[:, :])
                elif kind == "gate":
                    b = step[1]
                    after([s for s in PLAN if s[:3] == ("x_turn", "cross", b)][0])
                    c = 1 + (b % BPT) * P
                    for k in range(DK):
                        mm = pe.matmul(g[:, 0:E], xn_t[:, k, c:c + P], gate_sb[:, k, :],
                                       start=(k == 0), stop=(k == DK - 1))
                mm.then_inc(g_full, 1)

            g = tail_bank(pe, "col_turn")
            pe.wait_ge(router_pe, 1)
            pe.transpose(g[0:E, 0:P], tmp16[:, 1, :], ident[:, :]).then_inc(g_full, 1)
            g = tail_bank(pe, "col_back")
            pe.wait_ge(router_pe, 2)
            pe.matmul(g[:, 0:E], turned[:, 0, :], ident[0:E, 0:E], start=True, stop=True).then_inc(g_full, 1)
            pe.wait_ge(const_ready, 6)
            for it in range(SINK_ITERS):
                g = tail_bank(pe, ("col_sum", it))
                pe.wait_ge(router_pe, 3 + it)
                pe.matmul(g[:, 0:E], ones[:, :], tmp16[:, 1, :], start=True, stop=True).then_inc(g_full, 1)
            g = tail_bank(pe, "aff")
            pe.wait_ge(router_pe, 4 + SINK_ITERS)
            pe.transpose(g[:, 0:P], affin_r[:, 0:P], ident[:, :])
            pe.transpose(g[:, P:2 * P], affin_r[:, P:2 * P], ident[:, :]).then_inc(g_full, 1)
            pe.wait_ge(router_pe, 5 + SINK_ITERS)
            for name, best in (("cand_v", best_v), ("cand_i", best_f)):
                g = tail_bank(pe, name)
                for c in range(NCH):
                    mm = pe.matmul(g[0:E, c * CAP:(c + 1) * CAP], ident[:, c * E:(c + 1) * E], best,
                                   start=True, stop=True)
                mm.then_inc(g_full, 1)
            g = tail_bank(pe, "tops")
            pe.wait_ge(router_pe, 6 + SINK_ITERS)
            pe.transpose(g[0:CAP, 0:E], tops[:, 2, :], ident[0:E, 0:E]).then_inc(g_full, 1)

            def expert_in(i):
                g = tail_bank(pe, ("xe", i))
                pe.wait_ge(gathered[i], 16)
                for k in range(DK):
                    mm = pe.transpose(g[:, k * P:(k + 1) * P], x_e[i][:, k * P:(k + 1) * P], ident[:, :])
                mm.then_inc(g_full, 1)

            def hidden(i):
                for e in range(2):
                    n = 2 * i + e
                    pe.wait_ge(w1_loaded[n % NSLOT], 16 * (n // NSLOT + 1))
                pe.wait_ge(g_free, TG["xe", i] + 1)
                for f in range(2):
                    g = tail_bank(pe, ("h", i, f))
                    for k in range(DK):
                        for e in range(2):
                            w = slots[(2 * i + e) % NSLOT][:, 0:2048].rearrange("p (k n) -> p k n", k=DK)
                            mm = pe.matmul(g[CAP * e:CAP * (e + 1), :], x_et[i % 2][:, k, CAP * e:CAP * (e + 1)],
                                           w[:, k, f * TILE:(f + 1) * TILE], start=(k == 0), stop=(k == DK - 1))
                    mm.then_inc(g_full, 1)

            def turn_hidden(i):
                pe.wait_ge(g_free, TG["h", i, 1] + 1)
                if i >= 2:
                    pe.wait_ge(gelu_done, i - 1)
                else:
                    pe.wait_ge(exp_done, 2 * len(QUADS))
                pt = ps[i % 2][:, :, :].rearrange("p a b -> p (a b)")
                for f in range(8):
                    mm = pe.transpose(pt[:, f * P:(f + 1) * P], h_sb[i % 2][:, f * P:(f + 1) * P], ident[:, :])
                mm.then_inc(h_turned, 1)

            def expert_out(i):
                g = tail_bank(pe, ("y", i))
                pe.wait_ge(gelu_done, i + 1)
                for n in range(2 * i, 2 * i + 2):
                    pe.wait_ge(w2_loaded[n % NSLOT], 16 * (n // NSLOT + 1))
                for f in range(8):
                    for e in range(2):
                        w = slots[(2 * i + e) % NSLOT][:, 2048:4096].rearrange("p (k n) -> p k n", k=8)
                        mm = pe.matmul(g[CAP * e:CAP * (e + 1), 0:D],
                                       h_t[i % 2][:, f * P + CAP * e:f * P + CAP * (e + 1)], w[:, f, :],
                                       start=(f == 0), stop=(f == 7))
                mm.then_inc(g_full, 1)

            expert_in(0)
            hidden(0)
            for i in range(E // 2):
                turn_hidden(i)
                if i + 1 < E // 2:
                    expert_in(i + 1)
                    hidden(i + 1)
                expert_out(i)


def kernel(**inputs):
    import numpy as np
    import concourse.bacc as bacc
    from concourse.bass_utils import run_bass_kernel_spmd

    def turned(name):
        return np.ascontiguousarray(np.asarray(inputs[name]).T)

    def array(name):
        return np.ascontiguousarray(np.asarray(inputs[name]))

    w1q, w2q = turned("L0_attn_W1_q"), turned("L0_attn_W2_q")
    layout = {
        "x": array("x").reshape(T, D),
        "ctx_t": np.ascontiguousarray(array("ctx_1024").reshape(S, D).T),
        "w_self": np.concatenate([w1q[:D], w2q[:D], turned("L0_attn_W1_k"), turned("L0_attn_W2_k"),
                                  turned("L0_attn_Wv"), w1q[D:], w2q[D:]], axis=1),
        "w_o": turned("L0_attn_Wo"),
        "w_xq": turned("L0_xattn_Wq"),
        "w_xk": turned("L0_xattn_Wk"),
        "w_xv": turned("L0_xattn_Wv"),
        "w_xo": turned("L0_xattn_Wo"),
        "bv": array("L0_attn_bv"),
        "bo": array("L0_attn_bo"),
        "xbo": array("L0_xattn_bo"),
        "gate_t": turned("L0_ffn_gate_query"),
        "log_temp": array("L0_ffn_log_temp").reshape(1),
        "w1": array("L0_ffn_w1"),
        "b1": array("L0_ffn_b1"),
        "w2": array("L0_ffn_w2"),
        "b2": array("L0_ffn_b2"),
    }
    nc = bacc.Bacc("TRN2", target_bir_lowering=False, num_devices=1)
    args = [nc.dram_tensor(f"in_{n}", a.shape, mybir.dt.from_np(a.dtype), kind="ExternalInput").ap()
            for n, a in layout.items()]
    out = nc.dram_tensor("out", (T, D), F32, kind="ExternalOutput").ap()
    decoder_layer(nc, *args, out)
    r = run_bass_kernel_spmd(nc, [{f"in_{n}": a for n, a in layout.items()}], core_ids=[0])
    return r.results[0]["out"].reshape(1, T, D)
```
